# Optimizing a Trainium2 kernel written in Bass

```python
import numpy as np
import jax
import jax.numpy as jnp

def _softmax(x, axis=-1):
    return jax.nn.softmax(x, axis=axis)

def _gelu(x):
    return jax.nn.gelu(x, approximate=True)

def _silu(x):
    return jax.nn.silu(x)

def _sigmoid(x):
    return jax.nn.sigmoid(x)

def _layernorm(x, axis=-1, eps=1e-05):
    m = jnp.mean(x, axis=axis, keepdims=True)
    v = jnp.var(x, axis=axis, keepdims=True)
    return (x - m) / jnp.sqrt(v + eps)

def _scatter_add(tgt, idx, src, axis=0):
    return tgt.at[idx].add(src)

def _segment_sum(src, seg, n):
    return jax.ops.segment_sum(src, seg, n)
kernel_name = 'mk_seq_preln_d1_jaxref_r4_b929b8'

def setup_inputs(seed: int=0):
    np.random.seed(seed)
    _w = jnp.asarray

    def _L0_attn_setup():
        import jax, jax.numpy as jnp
        import numpy as np
        DIM = 256
        D_STATE = 16
        D_CONV = 4
        EXPAND = 2
        D_INNER = EXPAND * DIM

        def _mamba_forward(x, W_in, conv_w, conv_b, W_x, W_dt, b_dt, A_log, D, W_out):
            b, seq_len, _ = x.shape
            x_and_res = x @ W_in.T
            xp, res = jnp.split(x_and_res, 2, axis=-1)
            xc = jnp.swapaxes(xp, 1, 2)
            xc = jax.lax.conv_general_dilated(xc, conv_w, window_strides=(1,), padding=[(D_CONV - 1, 0)], dimension_numbers=('NCH', 'OIH', 'NCH'), feature_group_count=D_INNER)
            xc = xc + conv_b[None, :, None]
            xc = jnp.swapaxes(xc, 1, 2)
            xc = jax.nn.silu(xc)
            ssm = xc @ W_x.T
            B = ssm[..., :D_STATE]
            C = ssm[..., D_STATE:2 * D_STATE]
            dt = ssm[..., 2 * D_STATE:]
            dt = jax.nn.softplus(dt @ W_dt.T + b_dt)
            A = -jnp.exp(A_log)

            def step(h, inp):
                xt, dt_t, B_t, C_t = inp
                A_disc = jnp.exp(A[None, None, :] * dt_t[:, :, None])
                h = A_disc * h + dt_t[:, :, None] * B_t[:, None, :] * xt[:, :, None]
                y_t = jnp.einsum('bed,bd->be', h, C_t) + D * xt
                return (h, y_t)
            h0 = jnp.zeros((b, D_INNER, D_STATE), dtype=x.dtype)
            xs = (jnp.swapaxes(xc, 0, 1), jnp.swapaxes(dt, 0, 1), jnp.swapaxes(B, 0, 1), jnp.swapaxes(C, 0, 1))
            _, ys = jax.lax.scan(step, h0, xs)
            y = jnp.swapaxes(ys, 0, 1)
            y = jax.nn.silu(y + res)
            return y @ W_out.T
        key = jax.random.key(seed)
        ks = jax.random.split(key, 9)
        b, seq = (2, 512)
        s = lambda k, shape, fan: jax.random.normal(k, shape, dtype=jnp.float32) * (1.0 / np.sqrt(fan))
        x = jax.random.normal(ks[0], (b, seq, DIM), dtype=jnp.float32)
        W_in = s(ks[1], (2 * D_INNER, DIM), DIM)
        conv_w = s(ks[2], (D_INNER, 1, D_CONV), D_CONV)
        conv_b = jnp.zeros((D_INNER,), dtype=jnp.float32)
        W_x = s(ks[3], (2 * D_STATE + 1, D_INNER), D_INNER)
        W_dt = s(ks[4], (D_INNER, 1), 1)
        b_dt = jnp.zeros((D_INNER,), dtype=jnp.float32)
        A_log = jnp.log(jnp.arange(1, D_STATE + 1, dtype=jnp.float32))
        D = jnp.ones((D_INNER,), dtype=jnp.float32)
        W_out = s(ks[5], (DIM, D_INNER), D_INNER)
        return {'x': x, 'W_in': W_in, 'conv_w': conv_w, 'conv_b': conv_b, 'W_x': W_x, 'W_dt': W_dt, 'b_dt': b_dt, 'A_log': A_log, 'D': D, 'W_out': W_out}
    _L0_attn_in = _L0_attn_setup()

    def _L0_ffn_setup():
        import jax, jax.numpy as jnp
        import numpy as np
        D_IN, D_HID = (256, 1024)

        def _ternary(key, shape):
            return jax.random.randint(key, shape, -1, 2).astype(jnp.float32)

        def _tlin(x, w, s):
            return jnp.einsum('bsi,oi->bso', x, w) * s
        key = jax.random.key(seed)
        ks = jax.random.split(key, 12)
        inv = lambda fan: 1.0 / np.sqrt(fan).astype(np.float32)
        return {'x': jax.random.normal(ks[0], (4, 512, D_IN), dtype=jnp.float32), 'w1_w': _ternary(ks[1], (D_HID, D_IN)), 'w1_s': jax.random.uniform(ks[2], (D_HID,), dtype=jnp.float32) * inv(D_IN), 'w2_w': _ternary(ks[3], (D_HID, D_IN)), 'w2_s': jax.random.uniform(ks[4], (D_HID,), dtype=jnp.float32) * inv(D_IN), 'h1_w': _ternary(ks[5], (D_HID, D_HID)), 'h1_s': jax.random.uniform(ks[6], (D_HID,), dtype=jnp.float32) * inv(D_HID), 'h2_w': _ternary(ks[7], (D_HID, D_HID)), 'h2_s': jax.random.uniform(ks[8], (D_HID,), dtype=jnp.float32) * inv(D_HID), 'w3_w': _ternary(ks[9], (D_IN, D_HID)), 'w3_s': jax.random.uniform(ks[10], (D_IN,), dtype=jnp.float32) * inv(D_HID)}
    _L0_ffn_in = _L0_ffn_setup()
    _d = {'L0_attn_x': _L0_attn_in['x'], 'L0_attn_W_in': _L0_attn_in['W_in'], 'L0_attn_conv_w': _L0_attn_in['conv_w'], 'L0_attn_conv_b': _L0_attn_in['conv_b'], 'L0_attn_W_x': _L0_attn_in['W_x'], 'L0_attn_W_dt': _L0_attn_in['W_dt'], 'L0_attn_b_dt': _L0_attn_in['b_dt'], 'L0_attn_A_log': _L0_attn_in['A_log'], 'L0_attn_D': _L0_attn_in['D'], 'L0_attn_W_out': _L0_attn_in['W_out'], 'L0_ffn_w1_w': _L0_ffn_in['w1_w'], 'L0_ffn_w1_s': _L0_ffn_in['w1_s'], 'L0_ffn_w2_w': _L0_ffn_in['w2_w'], 'L0_ffn_w2_s': _L0_ffn_in['w2_s'], 'L0_ffn_h1_w': _L0_ffn_in['h1_w'], 'L0_ffn_h1_s': _L0_ffn_in['h1_s'], 'L0_ffn_h2_w': _L0_ffn_in['h2_w'], 'L0_ffn_h2_s': _L0_ffn_in['h2_s'], 'L0_ffn_w3_w': _L0_ffn_in['w3_w'], 'L0_ffn_w3_s': _L0_ffn_in['w3_s']}
    _x0 = _d['L0_attn_x']
    _d['L0_attn_x'] = jax.random.normal(jax.random.fold_in(jax.random.key(seed), 1), (4, 2048, 256), dtype=_x0.dtype)
    del _x0
    return _d

def reference(L0_attn_x, L0_attn_W_in, L0_attn_conv_w, L0_attn_conv_b, L0_attn_W_x, L0_attn_W_dt, L0_attn_b_dt, L0_attn_A_log, L0_attn_D, L0_attn_W_out, L0_ffn_w1_w, L0_ffn_w1_s, L0_ffn_w2_w, L0_ffn_w2_s, L0_ffn_h1_w, L0_ffn_h1_s, L0_ffn_h2_w, L0_ffn_h2_s, L0_ffn_w3_w, L0_ffn_w3_s):

    def _L0_attn_ref(x, W_in, conv_w, conv_b, W_x, W_dt, b_dt, A_log, D, W_out):
        import jax, jax.numpy as jnp
        import numpy as np
        DIM = 256
        D_STATE = 16
        D_CONV = 4
        EXPAND = 2
        D_INNER = EXPAND * DIM

        def _mamba_forward(x, W_in, conv_w, conv_b, W_x, W_dt, b_dt, A_log, D, W_out):
            b, seq_len, _ = x.shape
            x_and_res = x @ W_in.T
            xp, res = jnp.split(x_and_res, 2, axis=-1)
            xc = jnp.swapaxes(xp, 1, 2)
            xc = jax.lax.conv_general_dilated(xc, conv_w, window_strides=(1,), padding=[(D_CONV - 1, 0)], dimension_numbers=('NCH', 'OIH', 'NCH'), feature_group_count=D_INNER)
            xc = xc + conv_b[None, :, None]
            xc = jnp.swapaxes(xc, 1, 2)
            xc = jax.nn.silu(xc)
            ssm = xc @ W_x.T
            B = ssm[..., :D_STATE]
            C = ssm[..., D_STATE:2 * D_STATE]
            dt = ssm[..., 2 * D_STATE:]
            dt = jax.nn.softplus(dt @ W_dt.T + b_dt)
            A = -jnp.exp(A_log)

            def step(h, inp):
                xt, dt_t, B_t, C_t = inp
                A_disc = jnp.exp(A[None, None, :] * dt_t[:, :, None])
                h = A_disc * h + dt_t[:, :, None] * B_t[:, None, :] * xt[:, :, None]
                y_t = jnp.einsum('bed,bd->be', h, C_t) + D * xt
                return (h, y_t)
            h0 = jnp.zeros((b, D_INNER, D_STATE), dtype=x.dtype)
            xs = (jnp.swapaxes(xc, 0, 1), jnp.swapaxes(dt, 0, 1), jnp.swapaxes(B, 0, 1), jnp.swapaxes(C, 0, 1))
            _, ys = jax.lax.scan(step, h0, xs)
            y = jnp.swapaxes(ys, 0, 1)
            y = jax.nn.silu(y + res)
            return y @ W_out.T
        return _mamba_forward(x, W_in, conv_w, conv_b, W_x, W_dt, b_dt, A_log, D, W_out)

    def _L0_ffn_ref(x, w1_w, w1_s, w2_w, w2_s, h1_w, h1_s, h2_w, h2_s, w3_w, w3_s):
        import jax, jax.numpy as jnp
        import numpy as np
        D_IN, D_HID = (256, 1024)

        def _ternary(key, shape):
            return jax.random.randint(key, shape, -1, 2).astype(jnp.float32)

        def _tlin(x, w, s):
            return jnp.einsum('bsi,oi->bso', x, w) * s
        h = jax.nn.silu(_tlin(x, w1_w, w1_s)) * _tlin(x, w2_w, w2_s)
        h = jax.nn.gelu(_tlin(h, h1_w, h1_s), approximate=False)
        h = jax.nn.gelu(_tlin(h, h2_w, h2_s), approximate=False)
        return _tlin(h, w3_w, w3_s)
    x = L0_attn_x
    x = x + _L0_attn_ref(_layernorm(x, axis=-1), L0_attn_W_in, L0_attn_conv_w, L0_attn_conv_b, L0_attn_W_x, L0_attn_W_dt, L0_attn_b_dt, L0_attn_A_log, L0_attn_D, L0_attn_W_out)
    x = x + _L0_ffn_ref(_layernorm(x, axis=-1), L0_ffn_w1_w, L0_ffn_w1_s, L0_ffn_w2_w, L0_ffn_w2_s, L0_ffn_h1_w, L0_ffn_h1_s, L0_ffn_h2_w, L0_ffn_h2_s, L0_ffn_w3_w, L0_ffn_w3_s)
    return x

_drawn_inputs = setup_inputs


def setup_inputs(seed=0):
    import zlib

    import numpy as np

    out = dict(_drawn_inputs(seed))
    spreads = {'L0_attn_conv_b': (0.0, 0.1), 'L0_attn_b_dt': (0.0, 0.1), 'L0_attn_D': (1.0, 0.2)}
    factors = {}
    for name, (base, spread) in spreads.items():
        noise = np.random.default_rng([zlib.crc32(name.encode()), seed]).standard_normal(out[name].shape)
        drawn = base * np.exp(spread * noise) if base else spread * noise
        out[name] = jnp.asarray(drawn.astype(out[name].dtype))
    for name, factor in factors.items():
        out[name] = (out[name] * factor).astype(out[name].dtype)
    return out
```

```python
from contextlib import ExitStack

import concourse.bass as bass
from concourse import mybir

F32 = mybir.dt.float32
ALU = mybir.AluOpType
ACT = mybir.ActivationFunctionType

P = 128
EPS = 1e-5
LOW = -40.0
HIGH = 40.0
T = 256
NT = T // P
TB = 512
NTB = TB // P


def program(nc, x, w_in, conv_w, conv_b, w_x, w_dt, b_dt, a_log, d_skip, w_out,
            w1, s1, w2, s2, h1, t1, h2, t2, w3, s3, x1_dram, out):
    BATCH, SEQ, DIM = x.shape
    DI = w_out.shape[0]
    TAPS = conv_w.shape[-1]
    NS = a_log.shape[0]
    HID = w1.shape[1]
    KD, ET, KH = DIM // P, DI // P, HID // P
    CHUNKS = BATCH * SEQ // T
    PER_SEQ = SEQ // T
    CB = BATCH * SEQ // TB
    HALO = TAPS - 1
    ROW_B, ROW_C, ROW_DT = 0, 32, 64
    assert DIM == 2 * P and DI == 4 * P and NT == 2 and NS % 2 == 0 and CHUNKS % 2 == 0 and CHUNKS >= 4

    x_rows = x.rearrange("b (c n p) d -> p (b c) n d", p=P, n=NT)
    x1_rows = x1_dram.rearrange("b (c n p) d -> p (b c) n d", p=P, n=NT)
    x1_rows_b = x1_dram.rearrange("b (c n p) d -> p (b c) n d", p=P, n=NTB)
    out_rows = out.rearrange("b (c n p) d -> p (b c) n d", p=P, n=NTB)

    with ExitStack() as ctx:
        def sb(name, shape, dt=F32, where=ctx):
            return where.enter_context(nc.sbuf_tensor(name, shape, dt))

        def sem(name):
            return ctx.enter_context(nc.semaphore(name))

        ident = sb("ident", [P, P])
        eps = sb("eps", [P, 1])
        w1_sb = sb("w1_sb", [P, KD, HID])
        w2_sb = sb("w2_sb", [P, KD, HID])
        h1_sb = sb("h1_sb", [P, KH, HID])
        h2_sb = sb("h2_sb", [P, KH, HID])
        w3_sb = sb("w3_sb", [P, KH, DIM])
        scales = sb("scales", [P, 4, KH])
        s3_row = sb("s3_row", [P, DIM])

        a_only = ctx.enter_context(ExitStack())
        w_in_sb = sb("w_in_sb", [P, KD, 2 * DI], where=a_only)
        w_x_sb = sb("w_x_sb", [P, ET, P], where=a_only)
        w_out_sb = sb("w_out_sb", [P, ET, DIM], where=a_only)
        conv_w_sb = sb("conv_w_sb", [P, ET, TAPS], where=a_only)
        conv_b_sb = sb("conv_b_sb", [P, ET], where=a_only)
        w_dt_sb = sb("w_dt_sb", [P, ET], where=a_only)
        b_dt_sb = sb("b_dt_sb", [P, ET], where=a_only)
        d_sb = sb("d_sb", [P, ET], where=a_only)
        neg_a = sb("neg_a", [P, NS], where=a_only)
        conv_diag = sb("conv_diag", [P, ET, TAPS, P], where=a_only)
        d_diag = sb("d_diag", [P, ET, P], where=a_only)
        keep = sb("keep", [P, CHUNKS + 1], where=a_only)
        keep_next = sb("keep_next", [P, 2], where=a_only)
        x_sb = sb("x_sb", [P, 2, NT, DIM], where=a_only)
        bn = sb("bn", [P, NT, 6], where=a_only)
        mv = sb("mv", [P, NT, 2], where=a_only)
        log_var = sb("log_var", [P, NT], where=a_only)
        rstd = sb("rstd", [P, NT], where=a_only)
        xn = sb("xn", [P, NT, DIM], where=a_only)
        xnT = sb("xnT", [P, KD, T], where=a_only)
        xp = sb("xp", [P, ET, HALO + T], where=a_only)
        sig = sb("sig", [P, ET, T], where=a_only)
        xc = sb("xc", [P, ET, T], where=a_only)
        ssm = sb("ssm", [P, 2, T], where=a_only)
        c_tok = sb("c_tok", [P, 2, NT, NS], where=a_only)
        z = sb("z", [P, ET, T], where=a_only)
        soft = sb("soft", [P, ET, T], where=a_only)
        dt = sb("dt", [P, 2, ET, T], where=a_only)
        u = sb("u", [P, 2, ET, T], where=a_only)
        b_row = sb("b_row", [P, 2, 2, T], where=a_only)
        ub = sb("ub", [P, 2, ET, T], where=a_only)
        h = sb("h", [P, 2, ET, T], where=a_only)
        carry = sb("carry", [P, NS, ET], where=a_only)
        acc = sb("acc", [P, 2, NT, DI], where=a_only)
        gsig = sb("gsig", [P, NT, DI], where=a_only)
        g = sb("g", [P, NT, DI], where=a_only)
        gT = gsig[:].rearrange("p n d -> p (n d)").rearrange("p (e t) -> p e t", t=T)
        x_res = sb("x_res", [P, 2, NT, DIM], where=a_only)
        x1_sb = sb("x1_sb", [P, 2, NT, DIM], where=a_only)
        a_only.close()

        xb = sb("xb", [P, 2, NTB, DIM])
        bn_b = sb("bn_b", [P, NTB, 6])
        mv_b = sb("mv_b", [P, NTB, 2])
        log_var_b = sb("log_var_b", [P, NTB])
        rstd_b = sb("rstd_b", [P, NTB])
        xn_b = sb("xn_b", [P, NTB, DIM])
        xnT_b = sb("xnT_b", [P, KD, TB])
        silu_b = sb("silu_b", [P, 2, TB])
        act1 = sb("act1", [P, KH, TB])
        act2 = sb("act2", [P, KH, TB])
        prod_b = sb("prod_b", [P, NTB, DIM])
        out_sb = sb("out_sb", [P, 2, NTB, DIM])

        banks = ctx.enter_context(nc.psum_tensor("banks", [P, 8, 512], F32))
        decay = [banks[:, 2 * s:2 * s + 2, :].rearrange("p b t -> p (b t)").rearrange("p (e t) -> p e t", t=T) for s in range(2)]
        turned = [banks[:, 4 + n, :] for n in range(NT)]
        front_bank = banks[:, 6, :]
        post_bank = banks[:, 7, :]
        ring = [banks[:, n, :] for n in range(6)]

        weights_in = sem("weights_in")
        mlp_weights_in = sem("mlp_weights_in")
        setup = sem("setup")
        a_ready = sem("a_ready")
        diag_ready = sem("diag_ready")
        x_in = sem("x_in")
        bn_done = sem("bn_done")
        stats_ready = sem("stats_ready")
        logvar_done = sem("logvar_done")
        rstd_ready = sem("rstd_ready")
        xn_ready = sem("xn_ready")
        front_full = sem("front_full")
        front_taken = sem("front_taken")
        halo_ready = sem("halo_ready")
        silu_step = sem("silu_step")
        xc_ready = sem("xc_ready")
        zmin_ready = sem("zmin_ready")
        soft_step = sem("soft_step")
        dt_ready = sem("dt_ready")
        u_ready = sem("u_ready")
        decay_ready = sem("decay_ready")
        ub_ready = sem("ub_ready")
        scan_done = sem("scan_done")
        carry_ready = sem("carry_ready")
        keep_ready = sem("keep_ready")
        turn_full = [sem(f"turn_full{n}") for n in range(NT)]
        y_added = [sem(f"y_added{n}") for n in range(NT)]
        gm_ready = sem("gm_ready")
        gate_step = sem("gate_step")
        g_ready = sem("g_ready")
        post_full = sem("post_full")
        post_taken = sem("post_taken")
        xres_in = sem("xres_in")
        x1_ready = sem("x1_ready")
        x1_out = sem("x1_out")

        def after(eng, s, value):
            if not (isinstance(value, int) and value <= 0):
                eng.wait_ge(s, value)

        FJ = 10
        F_XN, F_XP, F_CONV, F_SSM, F_C, F_DT, F_ACC = 0, 1, 3, 5, 6, 7, 8
        PE_FRONT = {2: 0, 3: 1, 4: 2, 5: 3, 6: 4, 9: 5, 10: 6, 11: 7, 12: 8, 14: 9}
        PE_POST = {5: 0, 7: 1, 9: 2}
        PJ = 3
        PAIRS = NS // 2

        def front_job(c, k):
            return FJ * c + k

        def post_bank_order(post, more):
            order = []
            for n in range(NS):
                if post and n in PE_POST:
                    order.append(("p", PE_POST[n]))
                if n % 2 == 0 and (more or n // 2 + 2 < PAIRS):
                    order.append(("b", n // 2 + 2))
            return {job: at for at, job in enumerate(order)}

        LONG, SHORT = PAIRS + PJ, PAIRS

        def post_bank_base(c):
            return 2 if isinstance(c, int) and c == 0 else 2 + SHORT + LONG * (c - 1)

        def post_bank_job(c, job):
            first, last = (isinstance(c, int) and c == n for n in (0, CHUNKS - 1))
            return post_bank_base(c) + post_bank_order(not first, not last)[job]

        def pair_job(c, k):
            if k >= 2:
                return post_bank_job(c, ("b", k))
            if isinstance(c, int) and c == 0:
                return k
            return post_bank_job(c - 1, ("b", PAIRS + k))

        def post_job(c, j):
            if isinstance(c, int) and c == CHUNKS - 1:
                return post_bank_base(c) + LONG - 2 + j
            return post_bank_job(c + 1, ("p", j))

        def bodies(front, scan, post, start, eng):
            def body(c, par, has_front, has_post):
                def between(n):
                    if has_post:
                        post(c - 1, 1 - par, n)
                    if has_front:
                        front(c + 1, 1 - par, n)
                scan(c, par, between, has_front)

            for n in range(NS):
                front(0, 0, n)
            start()
            body(0, 0, True, False)
            body(1, 1, True, True)
            with eng.Fori(1, CHUNKS // 2 - 1) as pair:
                body(2 * pair, 0, True, True)
                body(2 * pair + 1, 1, True, True)
            body(CHUNKS - 2, 0, True, True)
            body(CHUNKS - 1, 1, False, True)
            for n in range(NS):
                post(CHUNKS - 1, 1, n)

        def sigmoid(dst, src, ready, value, step, base, act):
            act.wait_ge(ready, value)
            nc.scalar.activation(dst, src, ACT.Exp, scale=-1.0).then_inc(step, 1)
            act.wait_ge(step, base + 1)
            nc.scalar.activation(dst, dst, ACT.Ln, bias=1.0).then_inc(step, 1)
            act.wait_ge(step, base + 2)
            nc.scalar.activation(dst, dst, ACT.Exp, scale=-1.0).then_inc(step, 1)

        RING = 6
        J_L1, J_H1 = 0, 2 * KH
        J_T = J_H1 + KH
        J_H2 = J_T + KD
        J_OUT = J_H2 + KH
        BJOBS = J_OUT + NTB // 2
        assert BJOBS % RING == 0
        xb_in = sem("xb_in")
        bn_b_done = sem("bn_b_done")
        stats_b_ready = sem("stats_b_ready")
        logvar_b_done = sem("logvar_b_done")
        rstd_b_ready = sem("rstd_b_ready")
        xn_b_ready = sem("xn_b_ready")
        ring_full = sem("ring_full")
        ring_taken = [sem(f"ring_taken{n}") for n in range(RING)]
        xnT_b_ready = sem("xnT_b_ready")
        silu_b_ready = sem("silu_b_ready")
        gated_ready = sem("gated_ready")
        hidden1_ready = sem("hidden1_ready")
        hidden2_ready = sem("hidden2_ready")
        prod_ready = sem("prod_ready")
        out_ready = sem("out_ready")
        out_stored = sem("out_stored")

        def ring_job(c, k):
            if isinstance(c, int) and c == CB - 1 and k >= J_H2:
                k -= KD
            return (KD + k) % RING, KD + BJOBS * c + k, BJOBS // RING * c + (KD + k) // RING

        def turn_job(c, d):
            return (d % RING, d, 0) if isinstance(c, int) and c == 0 else ring_job(c - 1, J_T + d)

        def bodies_b(eng, body):
            body(0, 0, True)
            body(1, 1, True)
            with eng.Fori(1, CB // 2 - 1) as pair:
                body(2 * pair, 0, True)
                body(2 * pair + 1, 1, True)
            body(CB - 2, 0, True)
            body(CB - 1, 1, False)

        block = ctx.enter_context(nc.Block())

        @block.sync
        def _(sp):
            sp.dma_start(w_in_sb[:], w_in.rearrange("(k p) n -> p k n", p=P)).then_inc(weights_in, 16)
            sp.dma_start(conv_w_sb[:], conv_w.rearrange("(e p) o k -> p e (o k)", p=P)).then_inc(weights_in, 16)
            for dst, src in ((conv_b_sb, conv_b), (w_dt_sb, w_dt), (b_dt_sb, b_dt), (d_sb, d_skip)):
                sp.dma_start(dst[:], src).then_inc(weights_in, 16)
            sp.dma_start(neg_a[:], a_log.rearrange("(o n) -> o n", o=1).to_broadcast([P, NS])).then_inc(weights_in, 16)
            sp.dma_start(w_out_sb[:], w_out.rearrange("(k p) n -> p k n", p=P)).then_inc(weights_in, 16)
            sp.wait_ge(setup, 6)
            w_x_rows = w_x.rearrange("(k p) n -> p k n", p=P)
            sp.dma_start(w_x_sb[:, :, ROW_B:ROW_B + NS], w_x_rows[:, :, 0:NS]).then_inc(weights_in, 16)
            sp.dma_start(w_x_sb[:, :, ROW_C:ROW_C + NS], w_x_rows[:, :, NS:2 * NS]).then_inc(weights_in, 16)
            with nc.allow_non_contiguous_dma(reason="the one column of dt, once"):
                sp.dma_start(w_x_sb[:, :, ROW_DT:ROW_DT + 1], w_x_rows[:, :, 2 * NS:]).then_inc(weights_in, 16)

            def both(first, first_value, second, second_value):
                values = [v if isinstance(v, int) else sp.snap(v) for v in (first_value, second_value)]
                sp.wait_ge(setup, 6)
                after(sp, first, values[0])
                after(sp, second, values[1])

            def load_x(c, par):
                both(xn_ready, c - 1, x_in, 16 * c)
                sp.dma_start(x_sb[:, par:par + 1], x_rows[:, bass.ds(c, 1)]).then_inc(x_in, 16)

            def load_res(c, par):
                both(x1_ready, c - 1, xres_in, 16 * c)
                sp.dma_start(x_res[:, par:par + 1], x_rows[:, bass.ds(c, 1)]).then_inc(xres_in, 16)

            def store_x1(c, par):
                both(x1_ready, c + 1, x1_out, 16 * c)
                sp.dma_start(x1_rows[:, bass.ds(c, 1)], x1_sb[:, par:par + 1]).then_inc(x1_out, 16)

            load_x(0, 0)
            load_x(1, 1)
            load_res(0, 0)
            load_res(1, 1)
            for dst, src in ((w1_sb, w1), (w2_sb, w2), (h1_sb, h1), (h2_sb, h2), (w3_sb, w3)):
                sp.dma_start(dst[:], src.rearrange("(k p) n -> p k n", p=P)).then_inc(mlp_weights_in, 16)
            for k, s in enumerate((s1, s2, t1, t2)):
                sp.dma_start(scales[:, k], s).then_inc(mlp_weights_in, 16)
            sp.dma_start(s3_row[:], s3.rearrange("(o n) -> o n", o=1).to_broadcast([P, DIM])).then_inc(mlp_weights_in, 16)
            load_x(2, 0)
            load_x(3, 1)
            with sp.Fori(1, CHUNKS // 2 - 1) as pair:
                for k in range(2):
                    c = 2 * pair + k
                    store_x1(c - 2, k)
                    load_res(c, k)
                    load_x(c + 2, k)
            for c in (CHUNKS - 2, CHUNKS - 1):
                store_x1(c - 2, c % 2)
                load_res(c, c % 2)
            for c in (CHUNKS - 2, CHUNKS - 1):
                store_x1(c, c % 2)
            sp.wait_ge(x1_out, 16 * CHUNKS)
            sp.wait_ge(carry_ready, NS * CHUNKS)

            def load_b(c, par):
                both(out_ready, c - 1, xb_in, 16 * c)
                sp.dma_start(xb[:, par:par + 1], x1_rows_b[:, bass.ds(c, 1)]).then_inc(xb_in, 16)

            def body(c, par, more):
                if more:
                    load_b(c + 1, 1 - par)
                both(out_ready, c + 1, out_stored, 16 * c)
                sp.dma_start(out_rows[:, bass.ds(c, 1)], out_sb[:, par:par + 1]).then_inc(out_stored, 16)

            load_b(0, 0)
            bodies_b(sp, body)
            sp.wait_ge(out_stored, 16 * CB)

        @block.gpsimd
        def _(pool):
            nc.gpsimd.memset(w_x_sb[:], 0.0).then_inc(setup, 1)
            nc.gpsimd.memset(ident[:], 1.0).then_inc(setup, 1)
            nc.gpsimd.memset(eps[:], EPS).then_inc(setup, 1)
            nc.gpsimd.memset(keep[:], 1.0).then_inc(setup, 1)
            nc.gpsimd.memset(carry[:], 0.0).then_inc(setup, 1)
            nc.gpsimd.memset(xp[:], 0.0).then_inc(setup, 1)
            pool.wait_ge(setup, 6)
            nc.gpsimd.affine_select(out=ident[:], in_=ident[:], compare_op=ALU.is_equal, fill=0.0, base=0,
                                    pattern=[[-1, P]], channel_multiplier=1).then_inc(setup, 1)
            nc.gpsimd.memset(keep[:, 0:CHUNKS:PER_SEQ], 0.0).then_inc(setup, 1)
            pool.wait_ge(setup, 8)

            def front(c, par, n):
                if n == NS - 1:
                    pool.wait_ge(dt_ready, c + 1)
                    nc.gpsimd.tensor_tensor(u[:, par], dt[:, par], xc[:], ALU.mult).then_inc(u_ready, 1)

            def scan(c, par, between, more):
                pool.wait_ge(u_ready, c + 1)
                pool.wait_ge(keep_ready, c + 1)

                def carry_out(n):
                    pool.wait_ge(scan_done, NS * c + n + 1)
                    nc.gpsimd.tensor_tensor(carry[:, n, :], h[:, n % 2, :, T - 1],
                                            keep_next[:, par:par + 1].to_broadcast([P, ET]), ALU.mult).then_inc(carry_ready, 1)

                for n in range(NS):
                    if n % 2 == 0:
                        pool.wait_ge(post_taken, pair_job(c, n // 2) + 1)
                    after(pool, scan_done, NS * c + n - 1)
                    nc.gpsimd.tensor_tensor(ub[:, n % 2], u[:, par],
                                            b_row[:, (n // 2) % 2, n % 2:n % 2 + 1, :].to_broadcast([P, ET, T]),
                                            ALU.mult).then_inc(ub_ready, 1)
                    if n >= 1:
                        carry_out(n - 1)
                    between(n)
                carry_out(NS - 1)

            bodies(front, scan, lambda c, par, n: None, lambda: None, pool)

        @block.scalar
        def _(act):
            nc.scalar.preload_act_table_set("natural_log_exp_and_others")
            act.wait_ge(weights_in, 16 * 11)
            nc.scalar.activation(neg_a[:], neg_a[:], ACT.Exp).then_inc(a_ready, 1)
            act.wait_ge(diag_ready, 1)
            act.wait_ge(setup, 8)

            def after_setup(s, value):
                value = value if isinstance(value, int) else act.snap(value)
                act.wait_ge(setup, 8)
                after(act, s, value)

            def take_front(c, k, dst, src):
                act.wait_ge(front_full, front_job(c, k) + 1)
                nc.scalar.activation(dst, src, ACT.Copy).then_inc(front_taken, 1)

            def take_acc(c, par, q):
                after(act, gm_ready, c - 1)
                take_front(c, F_ACC + q, acc[:, par, q], front_bank)

            def take_pair(c, k):
                act.wait_ge(post_full, pair_job(c, k) + 1)
                after(act, ub_ready, NS * c + 2 * k - 2)
                nc.scalar.activation(b_row[:, k % 2], post_bank.rearrange("p (n t) -> p n t", n=2), ACT.Copy).then_inc(post_taken, 1)

            def front(c, par, n):
                if n == 2:
                    act.wait_ge(stats_ready, c + 1)
                    nc.scalar.activation(log_var[:], mv[:, :, 1], ACT.Ln, bias=eps[:, 0:1]).then_inc(logvar_done, 1)
                    act.wait_ge(logvar_done, c + 1)
                    nc.scalar.activation(rstd[:], log_var[:], ACT.Exp, scale=-0.5).then_inc(rstd_ready, 1)
                if n == 4:
                    take_front(c, F_XN, xnT[:].rearrange("p k t -> p (k t)"), front_bank)
                if n == 5:
                    act.wait_ge(front_full, front_job(c, F_XP) + 1)
                    goes_on = keep[:, 0:1] if isinstance(c, int) and c == 0 else keep_next[:, 1 - par:2 - par]
                    after(act, keep_ready, c)
                    nc.scalar.activation(xp[:, :, 0:HALO], xp[:, :, T:T + HALO], ACT.Copy,
                                         scale=goes_on).then_inc(halo_ready, 1)
                    act.wait_ge(halo_ready, c + 1)
                if n in (5, 7):
                    j = (n - 5) // 2
                    take_front(c, F_XP + j, xp[:, 2 * j:2 * j + 2, HALO:], front_bank.rearrange("p (e t) -> p e t", e=2))
                if n == 9:
                    sigmoid(sig[:], xc[:], front_taken, front_job(c, F_CONV) + 2, silu_step, 3 * c, act)
                if n == 11:
                    take_front(c, F_SSM, ssm[:, par], front_bank[:, 0:T])
                if n == 12:
                    take_front(c, F_C, c_tok[:, par], front_bank[:, 0:NT * P].rearrange("p (n r) -> p n r", n=NT)[:, :, ROW_C:ROW_C + NS])
                if n == 14:
                    act.wait_ge(zmin_ready, c + 1)
                    nc.scalar.activation(soft[:], soft[:], ACT.Exp).then_inc(soft_step, 1)
                    act.wait_ge(soft_step, 2 * c + 1)
                    nc.scalar.activation(soft[:], soft[:], ACT.Ln, bias=1.0).then_inc(soft_step, 1)
                if n == 15:
                    take_acc(c, par, 0)
                    take_pair(c, 0)

            def post(c, par, n):
                if n == 3:
                    sigmoid(gsig[:], g[:], gm_ready, c + 1, gate_step, 3 * c, act)
                if n in (7, 9):
                    j = (n - 7) // 2
                    act.wait_ge(post_full, post_job(c, j) + 1)
                    nc.scalar.activation(gT[:, 2 * j:2 * j + 2], post_bank.rearrange("p (e t) -> p e t", e=2), ACT.Copy).then_inc(post_taken, 1)

            def scan(c, par, between, more):
                act.wait_ge(dt_ready, c + 1)
                after_setup(carry_ready, NS * (c - 1))
                nc.scalar.activation(keep_next[:, par:par + 1], keep[:, bass.ds(c + 1, 1)], ACT.Copy).then_inc(keep_ready, 1)
                for n in range(NS):
                    if n % 2 == 1:
                        take_pair(c, (n + 1) // 2) if n < NS - 1 else None
                    after(act, scan_done, NS * c + n - 1)
                    nc.scalar.activation(decay[n % 2], dt[:, par], ACT.Exp, scale=neg_a[:, n:n + 1]).then_inc(decay_ready, 1)
                    if n == 1:
                        take_acc(c, par, 1)
                    between(n)

            bodies(front, scan, post, lambda: None, act)

            act.wait_ge(mlp_weights_in, 16 * 10)

            def take(job, dst, func, scale, done):
                bank, place, of_bank = job
                act.wait_ge(ring_full, place + 1)
                nc.scalar.activation(dst, ring[bank], func, scale=scale).then_inc(ring_taken[bank], 1)
                act.wait_ge(ring_taken[bank], of_bank + 1)
                act.sem_inc(done, 1)

            def rstd_of(c):
                act.wait_ge(stats_b_ready, c + 1)
                nc.scalar.activation(log_var_b[:], mv_b[:, :, 1], ACT.Ln, bias=eps[:, 0:1]).then_inc(logvar_b_done, 1)
                act.wait_ge(logvar_b_done, c + 1)
                nc.scalar.activation(rstd_b[:], log_var_b[:], ACT.Exp, scale=-0.5).then_inc(rstd_b_ready, 1)

            def turned_rows(c):
                for d in range(KD):
                    take(turn_job(c, d), xnT_b[:, d], ACT.Copy, 1.0, xnT_b_ready)

            def body(c, par, more):
                for o in range(KH):
                    after(act, gated_ready, KH * c + o - 1)
                    take(ring_job(c, J_L1 + 2 * o), silu_b[:, o % 2], ACT.Silu, scales[:, 0, o:o + 1], silu_b_ready)
                if more:
                    rstd_of(c + 1)
                for o in range(KH):
                    take(ring_job(c, J_H1 + o), act2[:, o], ACT.Gelu, scales[:, 2, o:o + 1], hidden1_ready)
                if more:
                    turned_rows(c + 1)
                for o in range(KH):
                    take(ring_job(c, J_H2 + o), act1[:, o], ACT.Gelu, scales[:, 3, o:o + 1], hidden2_ready)

            rstd_of(0)
            turned_rows(0)
            bodies_b(act, body)

        @block.vector
        def _(dve):
            dve.wait_ge(weights_in, 16 * 11)
            dve.wait_ge(setup, 8)
            dve.wait_ge(a_ready, 1)
            nc.vector.tensor_scalar(neg_a[:], neg_a[:], -1.0, None, ALU.mult)
            for e in range(ET):
                for k in range(TAPS):
                    nc.vector.tensor_scalar(conv_diag[:, e, k], ident[:], conv_w_sb[:, e, k:k + 1], None, ALU.mult)
                last = nc.vector.tensor_scalar(d_diag[:, e], ident[:], d_sb[:, e:e + 1], None, ALU.mult)
            last.then_inc(diag_ready, 1)

            def front(c, par, n):
                if n == 0:
                    dve.wait_ge(x_in, 16 * (c + 1))
                    for q in range(NT):
                        last = nc.vector.bn_stats(bn[:, q], x_sb[:, par, q])
                    last.then_inc(bn_done, 1)
                    dve.wait_ge(setup, 8)
                    dve.wait_ge(bn_done, c + 1)
                    for q in range(NT):
                        last = nc.vector.bn_aggr(mv[:, q], bn[:, q])
                    last.then_inc(stats_ready, 1)
                if n == 1:
                    dve.wait_ge(rstd_ready, c + 1)
                    for q in range(NT):
                        last = nc.vector.tensor_scalar(xn[:, q], x_sb[:, par, q], mv[:, q, 0:1], rstd[:, q:q + 1],
                                                       ALU.subtract, ALU.mult)
                    last.then_inc(xn_ready, 1)
                if n in (6, 7):
                    j = n - 6
                    dve.wait_ge(front_full, front_job(c, F_CONV + j) + 1)
                    for i in range(2):
                        e = 2 * j + i
                        last = nc.vector.tensor_scalar(xc[:, e], front_bank[:, i * T:(i + 1) * T], conv_b_sb[:, e:e + 1],
                                                       LOW, ALU.add, ALU.max)
                    last.then_inc(front_taken, 1)
                if n == 8:
                    dve.wait_ge(silu_step, 3 * c + 3)
                    nc.vector.tensor_tensor(xc[:], xc[:], sig[:], ALU.mult).then_inc(xc_ready, 1)
                if n == 12:
                    dve.wait_ge(front_full, front_job(c, F_DT) + 1)
                    for e in range(ET):
                        last = nc.vector.tensor_scalar(z[:, e], front_bank[:, 0:T], w_dt_sb[:, e:e + 1], b_dt_sb[:, e:e + 1], ALU.mult, ALU.add)
                    last.then_inc(front_taken, 1)
                    dve.wait_ge(front_taken, front_job(c, F_DT) + 1)
                    nc.vector.tensor_scalar(soft[:], z[:], HIGH, None, ALU.min).then_inc(zmin_ready, 1)
                if n == 13:
                    dve.wait_ge(soft_step, 2 * c + 2)
                    nc.vector.tensor_tensor(dt[:, par], z[:], soft[:], ALU.max).then_inc(dt_ready, 1)

            def post(c, par, n):
                if n == 1:
                    for q in range(NT):
                        dve.wait_ge(y_added[q], NS * (c + 1))
                    nc.vector.tensor_scalar(g[:], acc[:, par], LOW, None, ALU.max).then_inc(gm_ready, 1)
                if n == 3:
                    dve.wait_ge(gate_step, 3 * c + 3)
                    nc.vector.tensor_tensor(g[:], g[:], gsig[:], ALU.mult).then_inc(g_ready, 1)
                if n == 10:
                    dve.wait_ge(post_full, post_job(c, 2) + 1)
                    dve.wait_ge(xres_in, 16 * (c + 1))
                    after(dve, x1_out, 16 * (c - 1))
                    nc.vector.tensor_tensor(x1_sb[:, par].rearrange("p n d -> p (n d)"), post_bank,
                                            x_res[:, par].rearrange("p n d -> p (n d)"), ALU.add).then_inc(x1_ready, 1)
                    dve.wait_ge(x1_ready, c + 1)
                    dve.sem_inc(post_taken, 1)

            def scan(c, par, between, more):
                def recur(n):
                    dve.wait_ge(decay_ready, NS * c + n + 1)
                    dve.wait_ge(ub_ready, NS * c + n + 1)
                    for q in range(NT):
                        after(dve, turn_full[q], NS * c + n - 1)
                    after(dve, carry_ready, NS * c + n - 1)
                    for e in range(ET):
                        last = nc.vector.tensor_tensor_scan(h[:, n % 2, e], decay[n % 2][:, e], ub[:, n % 2, e],
                                                            carry[:, n, e:e + 1], ALU.mult, ALU.add)
                    last.then_inc(scan_done, 1)

                def add_y(n):
                    for q in range(NT):
                        if n == 0:
                            dve.wait_ge(front_taken, front_job(c, F_ACC) + q + 1)
                        dve.wait_ge(turn_full[q], NS * c + n + 1)
                        after(dve, y_added[q], NS * c + n)
                        nc.vector.scalar_tensor_tensor(out=acc[:, par, q], in0=turned[q], scalar=c_tok[:, par, q, n:n + 1], in1=acc[:, par, q],
                                                       op0=ALU.mult, op1=ALU.add).then_inc(y_added[q], 1)

                recur(0)
                for n in range(NS):
                    if n + 1 < NS:
                        recur(n + 1)
                    add_y(n)
                    between(n)

            bodies(front, scan, post, lambda: None, dve)

            dve.wait_ge(mlp_weights_in, 16 * 10)

            def stats_b(c, par):
                dve.wait_ge(xb_in, 16 * (c + 1))
                for q in range(NTB):
                    last = nc.vector.bn_stats(bn_b[:, q], xb[:, par, q])
                last.then_inc(bn_b_done, 1)
                dve.wait_ge(setup, 8)
                dve.wait_ge(bn_b_done, c + 1)
                for q in range(NTB):
                    last = nc.vector.bn_aggr(mv_b[:, q], bn_b[:, q])
                last.then_inc(stats_b_ready, 1)

            def normalize_b(c, par):
                dve.wait_ge(rstd_b_ready, c + 1)
                for q in range(NTB):
                    last = nc.vector.tensor_scalar(xn_b[:, q], xb[:, par, q], mv_b[:, q, 0:1], rstd_b[:, q:q + 1],
                                                   ALU.subtract, ALU.mult)
                last.then_inc(xn_b_ready, 1)

            def body(c, par, more):
                if more:
                    stats_b(c + 1, 1 - par)
                for o in range(KH):
                    bank, place, of_bank = ring_job(c, J_L1 + 2 * o + 1)
                    dve.wait_ge(silu_b_ready, KH * c + o + 1)
                    dve.wait_ge(ring_full, place + 1)
                    nc.vector.scalar_tensor_tensor(out=act1[:, o], in0=ring[bank], scalar=scales[:, 1, o:o + 1], in1=silu_b[:, o % 2],
                                                   op0=ALU.mult, op1=ALU.mult).then_inc(ring_taken[bank], 1)
                    dve.wait_ge(ring_taken[bank], of_bank + 1)
                    dve.sem_inc(gated_ready, 1)
                if more:
                    normalize_b(c + 1, 1 - par)
                for j in range(NTB // 2):
                    bank, place, of_bank = ring_job(c, J_OUT + j)
                    dve.wait_ge(ring_full, place + 1)
                    nc.vector.tensor_tensor(prod_b[:, 2 * j:2 * j + 2], ring[bank].rearrange("p (n d) -> p n d", n=2),
                                            s3_row[:].rearrange("p (o d) -> p o d", o=1).to_broadcast([P, 2, DIM]),
                                            ALU.mult).then_inc(ring_taken[bank], 1)
                    dve.wait_ge(ring_taken[bank], of_bank + 1)
                after(dve, out_stored, 16 * (c - 1))
                nc.vector.tensor_tensor(out_sb[:, par], prod_b[:], xb[:, par], ALU.add).then_inc(out_ready, 1)

            stats_b(0, 0)
            normalize_b(0, 0)
            bodies_b(dve, body)

        @block.tensor
        def _(pe):
            pe.wait_ge(weights_in, 16 * 11)
            pe.wait_ge(setup, 8)
            pe.wait_ge(diag_ready, 1)

            def select(row):
                return ident[:, row:row + 1].to_broadcast([P, P])

            def front(c, par, n):
                job = PE_FRONT.get(n)
                if job is None:
                    return
                after(pe, front_taken, front_job(c, job))
                if job == F_XN:
                    pe.wait_ge(xn_ready, c + 1)
                    for q in range(NT):
                        for d in range(KD):
                            last = nc.tensor.transpose(front_bank[:, d * T + q * P:d * T + (q + 1) * P], xn[:, q, d * P:(d + 1) * P], ident[:])
                elif job < F_CONV:
                    for j in range(2):
                        e = 2 * (job - F_XP) + j
                        for d in range(KD):
                            last = nc.tensor.matmul(front_bank[:, j * T:(j + 1) * T], w_in_sb[:, d, e * P:(e + 1) * P], xnT[:, d],
                                                    start=(d == 0), stop=(d == KD - 1))
                elif job < F_SSM:
                    for j in range(2):
                        e = 2 * (job - F_CONV) + j
                        for tap in range(TAPS):
                            last = nc.tensor.matmul(front_bank[:, j * T:(j + 1) * T], conv_diag[:, e, tap], xp[:, e, tap:tap + T],
                                                    start=(tap == 0), stop=(tap == TAPS - 1))
                elif job == F_SSM:
                    pe.wait_ge(xc_ready, c + 1)
                    for e in range(ET):
                        last = nc.tensor.matmul(front_bank[:, 0:T], w_x_sb[:, e], xc[:, e], start=(e == 0), stop=(e == ET - 1))
                elif job == F_C:
                    for q in range(NT):
                        last = nc.tensor.transpose(front_bank[:, q * P:(q + 1) * P], ssm[:, par, q * P:(q + 1) * P], ident[:])
                elif job == F_DT:
                    last = nc.tensor.matmul(front_bank[:, 0:T], select(ROW_DT), ssm[:, par], start=True, stop=True)
                else:
                    q = job - F_ACC
                    for d in range(KD):
                        nc.tensor.matmul(front_bank, xnT[:, d, q * P:(q + 1) * P], w_in_sb[:, d, DI:2 * DI], start=(d == 0), stop=False)
                    for e in range(ET):
                        last = nc.tensor.matmul(front_bank[:, e * P:(e + 1) * P], xc[:, e, q * P:(q + 1) * P], d_diag[:, e],
                                                start=False, stop=(e == ET - 1))
                last.then_inc(front_full, 1)

            def post(c, par, n):
                job = PE_POST.get(n)
                if job is None:
                    return
                pe.wait_ge(post_taken, post_job(c, job))
                if job < 2:
                    pe.wait_ge(g_ready, c + 1)
                    for i in range(2):
                        e = 2 * job + i
                        for q in range(NT):
                            last = nc.tensor.transpose(post_bank[:, i * T + q * P:i * T + (q + 1) * P], g[:, q, e * P:(e + 1) * P], ident[:])
                else:
                    for q in range(NT):
                        for e in range(ET):
                            last = nc.tensor.matmul(post_bank[:, q * DIM:(q + 1) * DIM], gT[:, e, q * P:(q + 1) * P], w_out_sb[:, e],
                                                    start=(e == 0), stop=(e == ET - 1))
                last.then_inc(post_full, 1)

            def pair_rows(c, par, k):
                after(pe, post_taken, pair_job(c, k))
                for j in range(2):
                    last = nc.tensor.matmul(post_bank[:, j * T:(j + 1) * T], select(ROW_B + 2 * k + j), ssm[:, par], start=True, stop=True)
                last.then_inc(post_full, 1)

            def scan(c, par, between, more):
                for n in range(NS):
                    pe.wait_ge(scan_done, NS * c + n + 1)
                    for q in range(NT):
                        after(pe, y_added[q], NS * c + n)
                        for e in range(ET):
                            last = nc.tensor.transpose(turned[q][:, e * P:(e + 1) * P], h[:, n % 2, e, q * P:(q + 1) * P], ident[:])
                        last.then_inc(turn_full[q], 1)
                    between(n)
                    if n % 2 == 0:
                        k = n // 2 + 2
                        if k < PAIRS:
                            pair_rows(c, par, k)
                        elif more:
                            pair_rows(c + 1, 1 - par, k - PAIRS)

            def start():
                pair_rows(0, 0, 0)
                pair_rows(0, 0, 1)

            bodies(front, scan, post, start, pe)

            pe.wait_ge(mlp_weights_in, 16 * 10)

            def free(job):
                bank, place, of_bank = job
                after(pe, ring_taken[bank], of_bank)
                return ring[bank]

            def turn_rows(c):
                pe.wait_ge(xn_b_ready, c + 1)
                for d in range(KD):
                    bank = free(turn_job(c, d))
                    for q in range(NTB):
                        last = nc.tensor.transpose(bank[:, q * P:(q + 1) * P], xn_b[:, q, d * P:(d + 1) * P], ident[:])
                    last.then_inc(ring_full, 1)

            def layer(c, job0, weights, rows, rows_ready, count):
                first = RING // 2
                tiles = [list(range(first))] + [[o] for o in range(first, KH)]
                for group in tiles:
                    banks_of = [free(ring_job(c, job0 + o)) for o in group]
                    for k in range(KH):
                        if group[0] == 0:
                            pe.wait_ge(rows_ready, KH * c + k + 1)
                        for o, bank in zip(group, banks_of):
                            last = nc.tensor.matmul(bank, weights[:, k, o * P:(o + 1) * P], rows[:, k], start=(k == 0), stop=(k == KH - 1))
                            if k == KH - 1:
                                last.then_inc(ring_full, 1)

            def body(c, par, more):
                pe.wait_ge(xnT_b_ready, KD * (c + 1))
                for o in range(KH):
                    for i, weights in enumerate((w1_sb, w2_sb)):
                        bank = free(ring_job(c, J_L1 + 2 * o + i))
                        for d in range(KD):
                            last = nc.tensor.matmul(bank, weights[:, d, o * P:(o + 1) * P], xnT_b[:, d], start=(d == 0), stop=(d == KD - 1))
                        last.then_inc(ring_full, 1)
                layer(c, J_H1, h1_sb, act1, gated_ready, KH)
                if more:
                    turn_rows(c + 1)
                layer(c, J_H2, h2_sb, act2, hidden1_ready, KH)
                banks_of = [free(ring_job(c, J_OUT + j)) for j in range(NTB // 2)]
                for half in range(2):
                    for k in range(KH):
                        if half == 0:
                            pe.wait_ge(hidden2_ready, KH * c + k + 1)
                        for j, bank in enumerate(banks_of):
                            q = 2 * j + half
                            last = nc.tensor.matmul(bank[:, half * DIM:(half + 1) * DIM], act1[:, k, q * P:(q + 1) * P], w3_sb[:, k],
                                                    start=(k == 0), stop=(k == KH - 1))
                            if half == 1 and k == KH - 1:
                                last.then_inc(ring_full, 1)

            turn_rows(0)
            bodies_b(pe, body)


_INS = ["x", "w_in", "conv_w", "conv_b", "w_x", "w_dt", "b_dt", "a_log", "d_skip", "w_out",
        "w1", "s1", "w2", "s2", "h1", "t1", "h2", "t2", "w3", "s3"]


def kernel(**inputs):
    import numpy as np
    import concourse.bacc as bacc
    from concourse.bass_utils import run_bass_kernel_spmd

    a = {k[3:]: np.asarray(v) for k, v in inputs.items()}

    def turn(w):
        return np.ascontiguousarray(w.T)

    def columns(v):
        return np.ascontiguousarray(v.reshape(-1, P).T)

    arrays = {
        "x": a["attn_x"], "w_in": turn(a["attn_W_in"]), "conv_w": a["attn_conv_w"], "conv_b": columns(a["attn_conv_b"]),
        "w_x": turn(a["attn_W_x"]), "w_dt": columns(a["attn_W_dt"]), "b_dt": columns(a["attn_b_dt"]),
        "a_log": a["attn_A_log"], "d_skip": columns(a["attn_D"]), "w_out": turn(a["attn_W_out"]),
        "w1": turn(a["ffn_w1_w"]), "s1": columns(a["ffn_w1_s"]), "w2": turn(a["ffn_w2_w"]), "s2": columns(a["ffn_w2_s"]),
        "h1": turn(a["ffn_h1_w"]), "t1": columns(a["ffn_h1_s"]), "h2": turn(a["ffn_h2_w"]), "t2": columns(a["ffn_h2_s"]),
        "w3": turn(a["ffn_w3_w"]), "s3": a["ffn_w3_s"],
    }
    nc = bacc.Bacc("TRN2", target_bir_lowering=False, num_devices=1)
    args = [nc.dram_tensor(f"in_{k}", arrays[k].shape, mybir.dt.from_np(arrays[k].dtype), kind="ExternalInput").ap() for k in _INS]
    x1 = nc.dram_tensor("x1_scratch", arrays["x"].shape, F32, kind="Internal").ap()
    out = nc.dram_tensor("out", arrays["x"].shape, F32, kind="ExternalOutput").ap()
    program(nc, *args, x1, out)
    r = run_bass_kernel_spmd(nc, [{f"in_{k}": arrays[k] for k in _INS}], core_ids=[0])
    return r.results[0]["out"]
```

```python
from contextlib import ExitStack

import concourse.bass as bass
from concourse import mybir

F32 = mybir.dt.float32
F32R = mybir.dt.float32r
I32 = mybir.dt.int32
ALU = mybir.AluOpType
ACT = mybir.ActivationFunctionType

P = 128
EPS = 1e-5
LOW = -40.0
HIGH = 40.0
T = 256
NT = T // P
TB = 512
NTB = TB // P


def program(nc, x, w_in, conv_w, conv_b, w_x, w_dt, b_dt, a_log, d_skip, w_out,
            w1, s1, w2, s2, h1, t1, h2, t2, w3, s3, x1_dram, out):
    BATCH, SEQ, DIM = x.shape
    DI = w_out.shape[0]
    TAPS = conv_w.shape[-1]
    NS = a_log.shape[0]
    HID = w1.shape[1]
    KD, ET, KH = DIM // P, DI // P, HID // P
    CHUNKS = BATCH * SEQ // T
    PER_SEQ = SEQ // T
    CB = BATCH * SEQ // TB
    HALO = TAPS - 1
    PIECE = NT * DI
    LOW_MASK = 0xFFF
    FLAG_STEPS = (2 * KD + 2 * KH + KH * DIM // HID) * HID // PIECE + 3
    ROW_B, ROW_C, ROW_DT = 0, 32, 64
    assert DIM == 2 * P and DI == 4 * P and NT == 2 and NS % 2 == 0 and CHUNKS % 2 == 0 and CHUNKS >= 4

    x_rows = x.rearrange("b (c n p) d -> p (b c) n d", p=P, n=NT)
    x1_rows = x1_dram.rearrange("b (c n p) d -> p (b c) n d", p=P, n=NT)
    x1_rows_b = x1_dram.rearrange("b (c n p) d -> p (b c) n d", p=P, n=NTB)
    out_rows = out.rearrange("b (c n p) d -> p (b c) n d", p=P, n=NTB)

    with ExitStack() as ctx:
        def sb(name, shape, dt=F32, where=ctx):
            return where.enter_context(nc.sbuf_tensor(name, shape, dt))

        def sem(name):
            return ctx.enter_context(nc.semaphore(name))

        ident = sb("ident", [P, P])
        eps = sb("eps", [P, 1])
        mlp_shapes = {"w1": [P, KD, HID], "w2": [P, KD, HID], "h1": [P, KH, HID], "h2": [P, KH, HID], "w3": [P, KH, DIM]}
        with ExitStack() as as_loaded:
            full = {name: sb(f"{name}_full", shape, where=as_loaded) for name, shape in mlp_shapes.items()}
        rounded = {name: sb(f"{name}_rounded", shape, F32R) for name, shape in mlp_shapes.items()}
        flag = sb("flag", [1, 1], I32)
        scales = sb("scales", [P, 4, KH])
        s3_row = sb("s3_row", [P, DIM])

        a_only = ctx.enter_context(ExitStack())
        w_in_sb = sb("w_in_sb", [P, KD, 2 * DI], where=a_only)
        w_x_sb = sb("w_x_sb", [P, ET, P], where=a_only)
        w_out_sb = sb("w_out_sb", [P, ET, DIM], where=a_only)
        conv_w_sb = sb("conv_w_sb", [P, ET, TAPS], where=a_only)
        conv_b_sb = sb("conv_b_sb", [P, ET], where=a_only)
        w_dt_sb = sb("w_dt_sb", [P, ET], where=a_only)
        b_dt_sb = sb("b_dt_sb", [P, ET], where=a_only)
        d_sb = sb("d_sb", [P, ET], where=a_only)
        neg_a = sb("neg_a", [P, NS], where=a_only)
        conv_diag = sb("conv_diag", [P, ET, TAPS, P], where=a_only)
        d_diag = sb("d_diag", [P, ET, P], where=a_only)
        keep = sb("keep", [P, CHUNKS + 1], where=a_only)
        keep_next = sb("keep_next", [P, 2], where=a_only)
        x_sb = sb("x_sb", [P, 2, NT, DIM], where=a_only)
        bn = sb("bn", [P, NT, 6], where=a_only)
        mv = sb("mv", [P, NT, 2], where=a_only)
        log_var = sb("log_var", [P, NT], where=a_only)
        rstd = sb("rstd", [P, NT], where=a_only)
        xn = sb("xn", [P, NT, DIM], where=a_only)
        xnT = sb("xnT", [P, KD, T], where=a_only)
        xp = sb("xp", [P, ET, HALO + T], where=a_only)
        sig = sb("sig", [P, ET, T], where=a_only)
        xc = sb("xc", [P, ET, T], where=a_only)
        ssm = sb("ssm", [P, 2, T], where=a_only)
        c_tok = sb("c_tok", [P, 2, NT, NS], where=a_only)
        z = sb("z", [P, ET, T], where=a_only)
        soft = sb("soft", [P, ET, T], where=a_only)
        dt = sb("dt", [P, 2, ET, T], where=a_only)
        u = sb("u", [P, 2, ET, T], where=a_only)
        b_row = sb("b_row", [P, 2, 2, T], where=a_only)
        ub = sb("ub", [P, 2, ET, T], where=a_only)
        h = sb("h", [P, 2, ET, T], where=a_only)
        carry = sb("carry", [P, NS, ET], where=a_only)
        acc = sb("acc", [P, 2, NT, DI], where=a_only)
        gsig = sb("gsig", [P, NT, DI], where=a_only)
        g = sb("g", [P, NT, DI], where=a_only)
        gT = gsig[:].rearrange("p n d -> p (n d)").rearrange("p (e t) -> p e t", t=T)
        low_bits = gsig[:].rearrange("p n d -> p (n d)").bitcast(I32)
        x_res = sb("x_res", [P, 2, NT, DIM], where=a_only)
        x1_sb = sb("x1_sb", [P, 2, NT, DIM], where=a_only)
        low_found = sb("low_found", [P, 1], I32, where=a_only)
        not_exact = sb("not_exact", [P, 1], where=a_only)
        ones = sb("ones", [P, 1], where=a_only)
        a_only.close()

        xb = sb("xb", [P, 2, NTB, DIM])
        bn_b = sb("bn_b", [P, NTB, 6])
        mv_b = sb("mv_b", [P, NTB, 2])
        log_var_b = sb("log_var_b", [P, NTB])
        rstd_b = sb("rstd_b", [P, NTB])
        xn_b = sb("xn_b", [P, NTB, DIM])
        silu_b = sb("silu_b", [P, 2, TB])
        prod_b = sb("prod_b", [P, NTB, DIM])
        out_sb = sb("out_sb", [P, 2, NTB, DIM])
        row_shapes = {"xnT_b": [P, KD, TB], "act1": [P, KH, TB], "act2": [P, KH, TB]}
        with ExitStack() as whole_only:
            whole = {name: sb(f"{name}_whole", shape, where=whole_only) for name, shape in row_shapes.items()}
        high = {name: sb(f"{name}_high", shape, F32R) for name, shape in row_shapes.items()}
        low = {name: sb(f"{name}_low", shape, F32R) for name, shape in row_shapes.items()}
        WIDE = 4
        wide = sb("wide", [P, WIDE, TB])

        banks = ctx.enter_context(nc.psum_tensor("banks", [P, 8, 512], F32))
        decay = [banks[:, 2 * s:2 * s + 2, :].rearrange("p b t -> p (b t)").rearrange("p (e t) -> p e t", t=T) for s in range(2)]
        turned = [banks[:, 4 + n, :] for n in range(NT)]
        front_bank = banks[:, 6, :]
        post_bank = banks[:, 7, :]
        ring = [banks[:, n, :] for n in range(6)]

        weights_in = sem("weights_in")
        mlp_weights_in = sem("mlp_weights_in")
        setup = sem("setup")
        a_ready = sem("a_ready")
        diag_ready = sem("diag_ready")
        x_in = sem("x_in")
        bn_done = sem("bn_done")
        stats_ready = sem("stats_ready")
        logvar_done = sem("logvar_done")
        rstd_ready = sem("rstd_ready")
        xn_ready = sem("xn_ready")
        front_full = sem("front_full")
        front_taken = sem("front_taken")
        halo_ready = sem("halo_ready")
        silu_step = sem("silu_step")
        xc_ready = sem("xc_ready")
        zmin_ready = sem("zmin_ready")
        soft_step = sem("soft_step")
        dt_ready = sem("dt_ready")
        u_ready = sem("u_ready")
        decay_ready = sem("decay_ready")
        ub_ready = sem("ub_ready")
        scan_done = sem("scan_done")
        carry_ready = sem("carry_ready")
        keep_ready = sem("keep_ready")
        turn_full = [sem(f"turn_full{n}") for n in range(NT)]
        y_added = [sem(f"y_added{n}") for n in range(NT)]
        gm_ready = sem("gm_ready")
        gate_step = sem("gate_step")
        g_ready = sem("g_ready")
        post_full = sem("post_full")
        post_taken = sem("post_taken")
        xres_in = sem("xres_in")
        x1_ready = sem("x1_ready")
        x1_out = sem("x1_out")

        def after(eng, s, value):
            if not (isinstance(value, int) and value <= 0):
                eng.wait_ge(s, value)

        FJ = 10
        F_XN, F_XP, F_CONV, F_SSM, F_C, F_DT, F_ACC = 0, 1, 3, 5, 6, 7, 8
        PE_FRONT = {2: 0, 3: 1, 4: 2, 5: 3, 6: 4, 9: 5, 10: 6, 11: 7, 12: 8, 14: 9}
        PE_POST = {5: 0, 7: 1, 9: 2}
        PJ = 3
        PAIRS = NS // 2

        def front_job(c, k):
            return FJ * c + k

        def post_bank_order(post, more):
            order = []
            for n in range(NS):
                if post and n in PE_POST:
                    order.append(("p", PE_POST[n]))
                if n % 2 == 0 and (more or n // 2 + 2 < PAIRS):
                    order.append(("b", n // 2 + 2))
            return {job: at for at, job in enumerate(order)}

        LONG, SHORT = PAIRS + PJ, PAIRS

        def post_bank_base(c):
            return 2 if isinstance(c, int) and c == 0 else 2 + SHORT + LONG * (c - 1)

        def post_bank_job(c, job):
            first, last = (isinstance(c, int) and c == n for n in (0, CHUNKS - 1))
            return post_bank_base(c) + post_bank_order(not first, not last)[job]

        def pair_job(c, k):
            if k >= 2:
                return post_bank_job(c, ("b", k))
            if isinstance(c, int) and c == 0:
                return k
            return post_bank_job(c - 1, ("b", PAIRS + k))

        def post_job(c, j):
            if isinstance(c, int) and c == CHUNKS - 1:
                return post_bank_base(c) + LONG - 2 + j
            return post_bank_job(c + 1, ("p", j))

        def bodies(front, scan, post, start, eng):
            def body(c, par, has_front, has_post):
                def between(n):
                    if has_post:
                        post(c - 1, 1 - par, n)
                    if has_front:
                        front(c + 1, 1 - par, n)
                scan(c, par, between, has_front)

            for n in range(NS):
                front(0, 0, n)
            start()
            body(0, 0, True, False)
            body(1, 1, True, True)
            with eng.Fori(1, CHUNKS // 2 - 1) as pair:
                body(2 * pair, 0, True, True)
                body(2 * pair + 1, 1, True, True)
            body(CHUNKS - 2, 0, True, True)
            body(CHUNKS - 1, 1, False, True)
            for n in range(NS):
                post(CHUNKS - 1, 1, n)

        def sigmoid(dst, src, ready, value, step, base, act):
            act.wait_ge(ready, value)
            nc.scalar.activation(dst, src, ACT.Exp, scale=-1.0).then_inc(step, 1)
            act.wait_ge(step, base + 1)
            nc.scalar.activation(dst, dst, ACT.Ln, bias=1.0).then_inc(step, 1)
            act.wait_ge(step, base + 2)
            nc.scalar.activation(dst, dst, ACT.Exp, scale=-1.0).then_inc(step, 1)

        RING = 6
        J_L1, J_H1 = 0, 2 * KH
        J_T = J_H1 + KH
        J_H2 = J_T + KD
        J_OUT = J_H2 + KH
        BJOBS = J_OUT + NTB // 2
        assert BJOBS % RING == 0
        xb_in = sem("xb_in")
        bn_b_done = sem("bn_b_done")
        stats_b_ready = sem("stats_b_ready")
        logvar_b_done = sem("logvar_b_done")
        rstd_b_ready = sem("rstd_b_ready")
        xn_b_ready = sem("xn_b_ready")
        ring_full = sem("ring_full")
        ring_taken = [sem(f"ring_taken{n}") for n in range(RING)]
        xnT_b_ready = sem("xnT_b_ready")
        silu_b_ready = sem("silu_b_ready")
        gated_ready = sem("gated_ready")
        hidden1_ready = sem("hidden1_ready")
        hidden2_ready = sem("hidden2_ready")
        prod_ready = sem("prod_ready")
        out_ready = sem("out_ready")
        out_stored = sem("out_stored")

        wide_ready = sem("wide_ready")
        high_ready = sem("high_ready")
        rows_split = sem("rows_split")
        flag_step = sem("flag_step")
        count_ready = sem("count_ready")
        flag_ready = sem("flag_ready")
        rounded_dve = sem("rounded_dve")
        rounded_pool = sem("rounded_pool")
        rounded_act = sem("rounded_act")

        S_H1, S_T, S_H2 = KH, 2 * KH, 2 * KH + KD
        SJOBS = 3 * KH + KD
        assert 2 * SJOBS % WIDE == 0 and (KD + SJOBS * -1 + S_T) % WIDE == 0

        def split_job(c, k):
            if isinstance(c, int) and c == CB - 1 and k >= S_H2:
                k -= KD
            return KD + SJOBS * c + k

        def split_turn(c, d):
            return d if isinstance(c, int) and c == 0 else split_job(c - 1, S_T + d)

        def wide_slot(par, k):
            return (KD + SJOBS * par + k) % WIDE

        def wide_turn_slot(par, d):
            return wide_slot(1 - par, S_T + d)

        def on_flag(eng, pass_b):
            eng.wait_ge(flag_ready, 1)
            value = eng.value_load(flag[0:1, 0:1])
            with eng.If(value == 0):
                pass_b(True)
            with eng.Else():
                pass_b(False)

        def ring_job(c, k):
            if isinstance(c, int) and c == CB - 1 and k >= J_H2:
                k -= KD
            return (KD + k) % RING, KD + BJOBS * c + k, BJOBS // RING * c + (KD + k) // RING

        def turn_job(c, d):
            return (d % RING, d, 0) if isinstance(c, int) and c == 0 else ring_job(c - 1, J_T + d)

        def bodies_b(eng, body):
            body(0, 0, True)
            body(1, 1, True)
            with eng.Fori(1, CB // 2 - 1) as pair:
                body(2 * pair, 0, True)
                body(2 * pair + 1, 1, True)
            body(CB - 2, 0, True)
            body(CB - 1, 1, False)

        block = ctx.enter_context(nc.Block())

        @block.sync
        def _(sp):
            sp.dma_start(w_in_sb[:], w_in.rearrange("(k p) n -> p k n", p=P)).then_inc(weights_in, 16)
            sp.dma_start(conv_w_sb[:], conv_w.rearrange("(e p) o k -> p e (o k)", p=P)).then_inc(weights_in, 16)
            for dst, src in ((conv_b_sb, conv_b), (w_dt_sb, w_dt), (b_dt_sb, b_dt), (d_sb, d_skip)):
                sp.dma_start(dst[:], src).then_inc(weights_in, 16)
            sp.dma_start(neg_a[:], a_log.rearrange("(o n) -> o n", o=1).to_broadcast([P, NS])).then_inc(weights_in, 16)
            sp.dma_start(w_out_sb[:], w_out.rearrange("(k p) n -> p k n", p=P)).then_inc(weights_in, 16)
            sp.wait_ge(setup, 6)
            w_x_rows = w_x.rearrange("(k p) n -> p k n", p=P)
            sp.dma_start(w_x_sb[:, :, ROW_B:ROW_B + NS], w_x_rows[:, :, 0:NS]).then_inc(weights_in, 16)
            sp.dma_start(w_x_sb[:, :, ROW_C:ROW_C + NS], w_x_rows[:, :, NS:2 * NS]).then_inc(weights_in, 16)
            with nc.allow_non_contiguous_dma(reason="the one column of dt, once"):
                sp.dma_start(w_x_sb[:, :, ROW_DT:ROW_DT + 1], w_x_rows[:, :, 2 * NS:]).then_inc(weights_in, 16)

            def both(first, first_value, second, second_value):
                values = [v if isinstance(v, int) else sp.snap(v) for v in (first_value, second_value)]
                sp.wait_ge(setup, 6)
                after(sp, first, values[0])
                after(sp, second, values[1])

            def load_x(c, par):
                both(xn_ready, c - 1, x_in, 16 * c)
                sp.dma_start(x_sb[:, par:par + 1], x_rows[:, bass.ds(c, 1)]).then_inc(x_in, 16)

            def load_res(c, par):
                both(x1_ready, c - 1, xres_in, 16 * c)
                sp.dma_start(x_res[:, par:par + 1], x_rows[:, bass.ds(c, 1)]).then_inc(xres_in, 16)

            def store_x1(c, par):
                both(x1_ready, c + 1, x1_out, 16 * c)
                sp.dma_start(x1_rows[:, bass.ds(c, 1)], x1_sb[:, par:par + 1]).then_inc(x1_out, 16)

            load_x(0, 0)
            load_x(1, 1)
            load_res(0, 0)
            load_res(1, 1)
            for dst, src in ((full["w1"], w1), (full["w2"], w2), (full["h1"], h1), (full["h2"], h2), (full["w3"], w3)):
                sp.dma_start(dst[:], src.rearrange("(k p) n -> p k n", p=P)).then_inc(mlp_weights_in, 16)
            for k, s in enumerate((s1, s2, t1, t2)):
                sp.dma_start(scales[:, k], s).then_inc(mlp_weights_in, 16)
            sp.dma_start(s3_row[:], s3.rearrange("(o n) -> o n", o=1).to_broadcast([P, DIM])).then_inc(mlp_weights_in, 16)
            load_x(2, 0)
            load_x(3, 1)
            with sp.Fori(1, CHUNKS // 2 - 1) as pair:
                for k in range(2):
                    c = 2 * pair + k
                    store_x1(c - 2, k)
                    load_res(c, k)
                    load_x(c + 2, k)
            for c in (CHUNKS - 2, CHUNKS - 1):
                store_x1(c - 2, c % 2)
                load_res(c, c % 2)
            for c in (CHUNKS - 2, CHUNKS - 1):
                store_x1(c, c % 2)
            sp.wait_ge(x1_out, 16 * CHUNKS)
            sp.wait_ge(carry_ready, NS * CHUNKS)

            def load_b(c, par):
                both(out_ready, c - 1, xb_in, 16 * c)
                sp.dma_start(xb[:, par:par + 1], x1_rows_b[:, bass.ds(c, 1)]).then_inc(xb_in, 16)

            def body(c, par, more):
                if more:
                    load_b(c + 1, 1 - par)
                both(out_ready, c + 1, out_stored, 16 * c)
                sp.dma_start(out_rows[:, bass.ds(c, 1)], out_sb[:, par:par + 1]).then_inc(out_stored, 16)

            def pass_b(exact):
                load_b(0, 0)
                bodies_b(sp, body)
                sp.wait_ge(out_stored, 16 * CB)

            on_flag(sp, pass_b)

        @block.gpsimd
        def _(pool):
            nc.gpsimd.memset(w_x_sb[:], 0.0).then_inc(setup, 1)
            nc.gpsimd.memset(ident[:], 1.0).then_inc(setup, 1)
            nc.gpsimd.memset(eps[:], EPS).then_inc(setup, 1)
            nc.gpsimd.memset(keep[:], 1.0).then_inc(setup, 1)
            nc.gpsimd.memset(carry[:], 0.0).then_inc(setup, 1)
            nc.gpsimd.memset(xp[:], 0.0).then_inc(setup, 1)
            pool.wait_ge(setup, 6)
            nc.gpsimd.affine_select(out=ident[:], in_=ident[:], compare_op=ALU.is_equal, fill=0.0, base=0,
                                    pattern=[[-1, P]], channel_multiplier=1).then_inc(setup, 1)
            nc.gpsimd.memset(keep[:, 0:CHUNKS:PER_SEQ], 0.0).then_inc(setup, 1)
            pool.wait_ge(setup, 8)

            def front(c, par, n):
                if n == NS - 1:
                    pool.wait_ge(dt_ready, c + 1)
                    nc.gpsimd.tensor_tensor(u[:, par], dt[:, par], xc[:], ALU.mult).then_inc(u_ready, 1)

            def scan(c, par, between, more):
                pool.wait_ge(u_ready, c + 1)
                pool.wait_ge(keep_ready, c + 1)

                def carry_out(n):
                    pool.wait_ge(scan_done, NS * c + n + 1)
                    nc.gpsimd.tensor_tensor(carry[:, n, :], h[:, n % 2, :, T - 1],
                                            keep_next[:, par:par + 1].to_broadcast([P, ET]), ALU.mult).then_inc(carry_ready, 1)

                for n in range(NS):
                    if n % 2 == 0:
                        pool.wait_ge(post_taken, pair_job(c, n // 2) + 1)
                    after(pool, scan_done, NS * c + n - 1)
                    nc.gpsimd.tensor_tensor(ub[:, n % 2], u[:, par],
                                            b_row[:, (n // 2) % 2, n % 2:n % 2 + 1, :].to_broadcast([P, ET, T]),
                                            ALU.mult).then_inc(ub_ready, 1)
                    if n >= 1:
                        carry_out(n - 1)
                    between(n)
                carry_out(NS - 1)

            bodies(front, scan, lambda c, par, n: None, lambda: None, pool)

            pool.wait_ge(mlp_weights_in, 16 * 10)

            def pass_b(exact):
                if exact:
                    nc.gpsimd.tensor_copy(rounded["h2"][:], full["h2"][:]).then_inc(rounded_pool, 1)

            on_flag(pool, pass_b)

        @block.scalar
        def _(act):
            nc.scalar.preload_act_table_set("natural_log_exp_and_others")
            act.wait_ge(weights_in, 16 * 11)
            nc.scalar.activation(neg_a[:], neg_a[:], ACT.Exp).then_inc(a_ready, 1)
            act.wait_ge(diag_ready, 1)
            act.wait_ge(setup, 8)

            def after_setup(s, value):
                value = value if isinstance(value, int) else act.snap(value)
                act.wait_ge(setup, 8)
                after(act, s, value)

            def take_front(c, k, dst, src):
                act.wait_ge(front_full, front_job(c, k) + 1)
                nc.scalar.activation(dst, src, ACT.Copy).then_inc(front_taken, 1)

            def take_acc(c, par, q):
                after(act, gm_ready, c - 1)
                take_front(c, F_ACC + q, acc[:, par, q], front_bank)

            def take_pair(c, k):
                act.wait_ge(post_full, pair_job(c, k) + 1)
                after(act, ub_ready, NS * c + 2 * k - 2)
                nc.scalar.activation(b_row[:, k % 2], post_bank.rearrange("p (n t) -> p n t", n=2), ACT.Copy).then_inc(post_taken, 1)

            def front(c, par, n):
                if n == 2:
                    act.wait_ge(stats_ready, c + 1)
                    nc.scalar.activation(log_var[:], mv[:, :, 1], ACT.Ln, bias=eps[:, 0:1]).then_inc(logvar_done, 1)
                    act.wait_ge(logvar_done, c + 1)
                    nc.scalar.activation(rstd[:], log_var[:], ACT.Exp, scale=-0.5).then_inc(rstd_ready, 1)
                if n == 4:
                    take_front(c, F_XN, xnT[:].rearrange("p k t -> p (k t)"), front_bank)
                if n == 5:
                    act.wait_ge(front_full, front_job(c, F_XP) + 1)
                    goes_on = keep[:, 0:1] if isinstance(c, int) and c == 0 else keep_next[:, 1 - par:2 - par]
                    after(act, keep_ready, c)
                    nc.scalar.activation(xp[:, :, 0:HALO], xp[:, :, T:T + HALO], ACT.Copy,
                                         scale=goes_on).then_inc(halo_ready, 1)
                    act.wait_ge(halo_ready, c + 1)
                if n in (5, 7):
                    j = (n - 5) // 2
                    take_front(c, F_XP + j, xp[:, 2 * j:2 * j + 2, HALO:], front_bank.rearrange("p (e t) -> p e t", e=2))
                if n == 9:
                    sigmoid(sig[:], xc[:], front_taken, front_job(c, F_CONV) + 2, silu_step, 3 * c, act)
                if n == 11:
                    take_front(c, F_SSM, ssm[:, par], front_bank[:, 0:T])
                if n == 12:
                    take_front(c, F_C, c_tok[:, par], front_bank[:, 0:NT * P].rearrange("p (n r) -> p n r", n=NT)[:, :, ROW_C:ROW_C + NS])
                if n == 14:
                    act.wait_ge(zmin_ready, c + 1)
                    nc.scalar.activation(soft[:], soft[:], ACT.Exp).then_inc(soft_step, 1)
                    act.wait_ge(soft_step, 2 * c + 1)
                    nc.scalar.activation(soft[:], soft[:], ACT.Ln, bias=1.0).then_inc(soft_step, 1)
                if n == 15:
                    take_acc(c, par, 0)
                    take_pair(c, 0)

            def post(c, par, n):
                if n == 3:
                    sigmoid(gsig[:], g[:], gm_ready, c + 1, gate_step, 3 * c, act)
                if n in (7, 9):
                    j = (n - 7) // 2
                    act.wait_ge(post_full, post_job(c, j) + 1)
                    nc.scalar.activation(gT[:, 2 * j:2 * j + 2], post_bank.rearrange("p (e t) -> p e t", e=2), ACT.Copy).then_inc(post_taken, 1)

            def scan(c, par, between, more):
                act.wait_ge(dt_ready, c + 1)
                after_setup(carry_ready, NS * (c - 1))
                nc.scalar.activation(keep_next[:, par:par + 1], keep[:, bass.ds(c + 1, 1)], ACT.Copy).then_inc(keep_ready, 1)
                for n in range(NS):
                    if n % 2 == 1:
                        take_pair(c, (n + 1) // 2) if n < NS - 1 else None
                    after(act, scan_done, NS * c + n - 1)
                    nc.scalar.activation(decay[n % 2], dt[:, par], ACT.Exp, scale=neg_a[:, n:n + 1]).then_inc(decay_ready, 1)
                    if n == 1:
                        take_acc(c, par, 1)
                    between(n)

            bodies(front, scan, post, lambda: None, act)

            act.wait_ge(mlp_weights_in, 16 * 10)

            def rstd_of(c):
                act.wait_ge(stats_b_ready, c + 1)
                nc.scalar.activation(log_var_b[:], mv_b[:, :, 1], ACT.Ln, bias=eps[:, 0:1]).then_inc(logvar_b_done, 1)
                act.wait_ge(logvar_b_done, c + 1)
                nc.scalar.activation(rstd_b[:], log_var_b[:], ACT.Exp, scale=-0.5).then_inc(rstd_b_ready, 1)

            def take(job, dst, func, scale, done):
                bank, place, of_bank = job
                act.wait_ge(ring_full, place + 1)
                nc.scalar.activation(dst, ring[bank], func, scale=scale).then_inc(ring_taken[bank], 1)
                act.wait_ge(ring_taken[bank], of_bank + 1)
                act.sem_inc(done, 1)

            def take_wide(job, row, slot, func, scale):
                after(act, rows_split, row - WIDE + 1)
                take(job, wide[:, slot], func, scale, wide_ready)

            def turned_rows(c, par, exact):
                for d in range(KD):
                    if exact:
                        take_wide(turn_job(c, d), split_turn(c, d), wide_turn_slot(par, d), ACT.Copy, 1.0)
                    else:
                        take(turn_job(c, d), whole["xnT_b"][:, d], ACT.Copy, 1.0, xnT_b_ready)

            def high_gated(c, par, o):
                row = split_job(c, o)
                act.wait_ge(wide_ready, row + 1)
                nc.scalar.activation(high["act1"][:, o], wide[:, wide_slot(par, o)], ACT.Copy).then_inc(high_ready, 1)

            def pass_b(exact):
                def body(c, par, more):
                    for o in range(KH):
                        if not exact:
                            after(act, gated_ready, KH * c + o - 1)
                        elif o >= 2:
                            act.wait_ge(wide_ready, split_job(c, o - 2) + 1)
                        take(ring_job(c, J_L1 + 2 * o), silu_b[:, o % 2], ACT.Silu, scales[:, 0, o:o + 1], silu_b_ready)
                        if exact and o >= 1:
                            high_gated(c, par, o - 1)
                    if exact:
                        high_gated(c, par, KH - 1)
                    if more:
                        rstd_of(c + 1)
                    for o in range(KH):
                        if exact:
                            take_wide(ring_job(c, J_H1 + o), split_job(c, S_H1 + o), wide_slot(par, S_H1 + o), ACT.Gelu, scales[:, 2, o:o + 1])
                        else:
                            take(ring_job(c, J_H1 + o), whole["act2"][:, o], ACT.Gelu, scales[:, 2, o:o + 1], hidden1_ready)
                    if more:
                        turned_rows(c + 1, 1 - par, exact)
                    for o in range(KH):
                        if exact:
                            slot = wide_slot(par, S_H2 + o - (0 if more else KD))
                            take_wide(ring_job(c, J_H2 + o), split_job(c, S_H2 + o), slot, ACT.Gelu, scales[:, 3, o:o + 1])
                        else:
                            take(ring_job(c, J_H2 + o), whole["act1"][:, o], ACT.Gelu, scales[:, 3, o:o + 1], hidden2_ready)

                if exact:
                    nc.scalar.activation(rounded["w3"][:], full["w3"][:], ACT.Copy).then_inc(rounded_act, 1)
                rstd_of(0)
                turned_rows(0, 0, exact)
                bodies_b(act, body)

            on_flag(act, pass_b)

        @block.vector
        def _(dve):
            dve.wait_ge(weights_in, 16 * 11)
            dve.wait_ge(setup, 8)
            dve.wait_ge(a_ready, 1)
            nc.vector.tensor_scalar(neg_a[:], neg_a[:], -1.0, None, ALU.mult)
            for e in range(ET):
                for k in range(TAPS):
                    nc.vector.tensor_scalar(conv_diag[:, e, k], ident[:], conv_w_sb[:, e, k:k + 1], None, ALU.mult)
                last = nc.vector.tensor_scalar(d_diag[:, e], ident[:], d_sb[:, e:e + 1], None, ALU.mult)
            last.then_inc(diag_ready, 1)

            def front(c, par, n):
                if n == 0:
                    dve.wait_ge(x_in, 16 * (c + 1))
                    for q in range(NT):
                        last = nc.vector.bn_stats(bn[:, q], x_sb[:, par, q])
                    last.then_inc(bn_done, 1)
                    dve.wait_ge(setup, 8)
                    dve.wait_ge(bn_done, c + 1)
                    for q in range(NT):
                        last = nc.vector.bn_aggr(mv[:, q], bn[:, q])
                    last.then_inc(stats_ready, 1)
                if n == 1:
                    dve.wait_ge(rstd_ready, c + 1)
                    for q in range(NT):
                        last = nc.vector.tensor_scalar(xn[:, q], x_sb[:, par, q], mv[:, q, 0:1], rstd[:, q:q + 1],
                                                       ALU.subtract, ALU.mult)
                    last.then_inc(xn_ready, 1)
                if n in (6, 7):
                    j = n - 6
                    dve.wait_ge(front_full, front_job(c, F_CONV + j) + 1)
                    for i in range(2):
                        e = 2 * j + i
                        last = nc.vector.tensor_scalar(xc[:, e], front_bank[:, i * T:(i + 1) * T], conv_b_sb[:, e:e + 1],
                                                       LOW, ALU.add, ALU.max)
                    last.then_inc(front_taken, 1)
                if n == 8:
                    dve.wait_ge(silu_step, 3 * c + 3)
                    nc.vector.tensor_tensor(xc[:], xc[:], sig[:], ALU.mult).then_inc(xc_ready, 1)
                if n == 12:
                    dve.wait_ge(front_full, front_job(c, F_DT) + 1)
                    for e in range(ET):
                        last = nc.vector.tensor_scalar(z[:, e], front_bank[:, 0:T], w_dt_sb[:, e:e + 1], b_dt_sb[:, e:e + 1], ALU.mult, ALU.add)
                    last.then_inc(front_taken, 1)
                    dve.wait_ge(front_taken, front_job(c, F_DT) + 1)
                    nc.vector.tensor_scalar(soft[:], z[:], HIGH, None, ALU.min).then_inc(zmin_ready, 1)
                if n == 13:
                    dve.wait_ge(soft_step, 2 * c + 2)
                    nc.vector.tensor_tensor(dt[:, par], z[:], soft[:], ALU.max).then_inc(dt_ready, 1)

            def post(c, par, n):
                if n == 1:
                    for q in range(NT):
                        dve.wait_ge(y_added[q], NS * (c + 1))
                    nc.vector.tensor_scalar(g[:], acc[:, par], LOW, None, ALU.max).then_inc(gm_ready, 1)
                if n == 3:
                    dve.wait_ge(gate_step, 3 * c + 3)
                    nc.vector.tensor_tensor(g[:], g[:], gsig[:], ALU.mult).then_inc(g_ready, 1)
                if n == 10:
                    dve.wait_ge(post_full, post_job(c, 2) + 1)
                    dve.wait_ge(xres_in, 16 * (c + 1))
                    after(dve, x1_out, 16 * (c - 1))
                    nc.vector.tensor_tensor(x1_sb[:, par].rearrange("p n d -> p (n d)"), post_bank,
                                            x_res[:, par].rearrange("p n d -> p (n d)"), ALU.add).then_inc(x1_ready, 1)
                    dve.wait_ge(x1_ready, c + 1)
                    dve.sem_inc(post_taken, 1)

            def scan(c, par, between, more):
                def recur(n):
                    dve.wait_ge(decay_ready, NS * c + n + 1)
                    dve.wait_ge(ub_ready, NS * c + n + 1)
                    for q in range(NT):
                        after(dve, turn_full[q], NS * c + n - 1)
                    after(dve, carry_ready, NS * c + n - 1)
                    for e in range(ET):
                        last = nc.vector.tensor_tensor_scan(h[:, n % 2, e], decay[n % 2][:, e], ub[:, n % 2, e],
                                                            carry[:, n, e:e + 1], ALU.mult, ALU.add)
                    last.then_inc(scan_done, 1)

                def add_y(n):
                    for q in range(NT):
                        if n == 0:
                            dve.wait_ge(front_taken, front_job(c, F_ACC) + q + 1)
                        dve.wait_ge(turn_full[q], NS * c + n + 1)
                        after(dve, y_added[q], NS * c + n)
                        nc.vector.scalar_tensor_tensor(out=acc[:, par, q], in0=turned[q], scalar=c_tok[:, par, q, n:n + 1], in1=acc[:, par, q],
                                                       op0=ALU.mult, op1=ALU.add).then_inc(y_added[q], 1)

                recur(0)
                for n in range(NS):
                    if n + 1 < NS:
                        recur(n + 1)
                    add_y(n)
                    between(n)
                    if isinstance(c, int) and c == 0 and n >= 2:
                        look_at_weights(2 * (n - 2))
                        look_at_weights(2 * (n - 2) + 1)

            pieces = [full[name][:].rearrange("p k n -> p (k n)")[:, at:at + PIECE].bitcast(I32)
                      for name, shape in mlp_shapes.items() for at in range(0, shape[1] * shape[2], PIECE)]
            assert len(pieces) + 2 <= 2 * NS - 2 and len(pieces) + 3 == FLAG_STEPS

            def look_at_weights(step):
                if step == 0:
                    dve.wait_ge(mlp_weights_in, 16 * 10)
                    nc.vector.tensor_tensor(low_bits, pieces[0], pieces[1], ALU.bitwise_or).then_inc(flag_step, 1)
                    nc.vector.memset(ones[:], 1.0).then_inc(flag_step, 1)
                    return
                last_or = len(pieces) - 2
                if step > last_or + 3:
                    return
                dve.wait_ge(flag_step, step + 1)
                if step <= last_or:
                    nc.vector.tensor_tensor(low_bits, low_bits, pieces[step + 1], ALU.bitwise_or).then_inc(flag_step, 1)
                elif step == last_or + 1:
                    nc.vector.tensor_scalar(low_bits, low_bits, LOW_MASK, None, ALU.bitwise_and).then_inc(flag_step, 1)
                elif step == last_or + 2:
                    nc.vector.tensor_reduce(low_found[:], low_bits, mybir.AxisListType.X, ALU.max).then_inc(flag_step, 1)
                else:
                    nc.vector.tensor_scalar(not_exact[:], low_found[:], 0.0, None, ALU.not_equal).then_inc(flag_step, 1)

            bodies(front, scan, post, lambda: None, dve)

            dve.wait_ge(count_ready, 1)
            nc.vector.tensor_copy(flag[:], ring[0][0:1, 0:1]).then_inc(flag_ready, 1)

            dve.wait_ge(mlp_weights_in, 16 * 10)

            def stats_b(c, par):
                dve.wait_ge(xb_in, 16 * (c + 1))
                for q in range(NTB):
                    last = nc.vector.bn_stats(bn_b[:, q], xb[:, par, q])
                last.then_inc(bn_b_done, 1)
                dve.wait_ge(setup, 8)
                dve.wait_ge(bn_b_done, c + 1)
                for q in range(NTB):
                    last = nc.vector.bn_aggr(mv_b[:, q], bn_b[:, q])
                last.then_inc(stats_b_ready, 1)

            def normalize_b(c, par):
                dve.wait_ge(rstd_b_ready, c + 1)
                for q in range(NTB):
                    last = nc.vector.tensor_scalar(xn_b[:, q], xb[:, par, q], mv_b[:, q, 0:1], rstd_b[:, q:q + 1],
                                                   ALU.subtract, ALU.mult)
                last.then_inc(xn_b_ready, 1)

            def gate(c, par, o, exact):
                bank, place, of_bank = ring_job(c, J_L1 + 2 * o + 1)
                dve.wait_ge(silu_b_ready, KH * c + o + 1)
                dve.wait_ge(ring_full, place + 1)
                if exact:
                    row = split_job(c, o)
                    after(dve, rows_split, row - WIDE + 1)
                    dst = wide[:, wide_slot(par, o)]
                else:
                    dst = whole["act1"][:, o]
                nc.vector.scalar_tensor_tensor(out=dst, in0=ring[bank], scalar=scales[:, 1, o:o + 1], in1=silu_b[:, o % 2],
                                               op0=ALU.mult, op1=ALU.mult).then_inc(ring_taken[bank], 1)
                dve.wait_ge(ring_taken[bank], of_bank + 1)
                dve.sem_inc(wide_ready if exact else gated_ready, 1)

            def take_high(row, slot, dst):
                dve.wait_ge(wide_ready, row + 1)
                nc.vector.tensor_copy(dst, wide[:, slot]).then_inc(high_ready, 1)

            def take_low(row, slot, high_part, dst):
                dve.wait_ge(high_ready, row + 1)
                nc.vector.tensor_tensor(dst, wide[:, slot], high_part.bitcast(F32), ALU.subtract).then_inc(rows_split, 1)

            def split(name, o, row, slot):
                take_high(row, slot, high[name][:, o])
                take_low(row, slot, high[name][:, o], low[name][:, o])

            def split_turned(c, par):
                for d in range(KD):
                    split("xnT_b", d, split_turn(c, d), wide_turn_slot(par, d))

            def low_gated(c, par, o):
                take_low(split_job(c, o), wide_slot(par, o), high["act1"][:, o], low["act1"][:, o])

            def pass_b(exact):
                def body(c, par, more):
                    if more:
                        stats_b(c + 1, 1 - par)
                    for o in range(KH):
                        gate(c, par, o, exact)
                        if exact and o >= 1:
                            low_gated(c, par, o - 1)
                    if exact:
                        low_gated(c, par, KH - 1)
                    if more:
                        normalize_b(c + 1, 1 - par)
                    if exact:
                        for o in range(KH):
                            split("act2", o, split_job(c, S_H1 + o), wide_slot(par, S_H1 + o))
                        if more:
                            split_turned(c + 1, 1 - par)
                        for o in range(KH):
                            split("act1", o, split_job(c, S_H2 + o), wide_slot(par, S_H2 + o - (0 if more else KD)))
                    for j in range(NTB // 2):
                        bank, place, of_bank = ring_job(c, J_OUT + j)
                        dve.wait_ge(ring_full, place + 1)
                        nc.vector.tensor_tensor(prod_b[:, 2 * j:2 * j + 2], ring[bank].rearrange("p (n d) -> p n d", n=2),
                                                s3_row[:].rearrange("p (o d) -> p o d", o=1).to_broadcast([P, 2, DIM]),
                                                ALU.mult).then_inc(ring_taken[bank], 1)
                        dve.wait_ge(ring_taken[bank], of_bank + 1)
                    after(dve, out_stored, 16 * (c - 1))
                    nc.vector.tensor_tensor(out_sb[:, par], prod_b[:], xb[:, par], ALU.add).then_inc(out_ready, 1)

                if exact:
                    for name in ("w1", "w2", "h1"):
                        nc.vector.tensor_copy(rounded[name][:], full[name][:]).then_inc(rounded_dve, 1)
                stats_b(0, 0)
                normalize_b(0, 0)
                if exact:
                    split_turned(0, 0)
                bodies_b(dve, body)

            on_flag(dve, pass_b)

        @block.tensor
        def _(pe):
            pe.wait_ge(weights_in, 16 * 11)
            pe.wait_ge(setup, 8)
            pe.wait_ge(diag_ready, 1)

            def select(row):
                return ident[:, row:row + 1].to_broadcast([P, P])

            def front(c, par, n):
                job = PE_FRONT.get(n)
                if job is None:
                    return
                after(pe, front_taken, front_job(c, job))
                if job == F_XN:
                    pe.wait_ge(xn_ready, c + 1)
                    for q in range(NT):
                        for d in range(KD):
                            last = nc.tensor.transpose(front_bank[:, d * T + q * P:d * T + (q + 1) * P], xn[:, q, d * P:(d + 1) * P], ident[:])
                elif job < F_CONV:
                    for j in range(2):
                        e = 2 * (job - F_XP) + j
                        for d in range(KD):
                            last = nc.tensor.matmul(front_bank[:, j * T:(j + 1) * T], w_in_sb[:, d, e * P:(e + 1) * P], xnT[:, d],
                                                    start=(d == 0), stop=(d == KD - 1))
                elif job < F_SSM:
                    for j in range(2):
                        e = 2 * (job - F_CONV) + j
                        for tap in range(TAPS):
                            last = nc.tensor.matmul(front_bank[:, j * T:(j + 1) * T], conv_diag[:, e, tap], xp[:, e, tap:tap + T],
                                                    start=(tap == 0), stop=(tap == TAPS - 1))
                elif job == F_SSM:
                    pe.wait_ge(xc_ready, c + 1)
                    for e in range(ET):
                        last = nc.tensor.matmul(front_bank[:, 0:T], w_x_sb[:, e], xc[:, e], start=(e == 0), stop=(e == ET - 1))
                elif job == F_C:
                    for q in range(NT):
                        last = nc.tensor.transpose(front_bank[:, q * P:(q + 1) * P], ssm[:, par, q * P:(q + 1) * P], ident[:])
                elif job == F_DT:
                    last = nc.tensor.matmul(front_bank[:, 0:T], select(ROW_DT), ssm[:, par], start=True, stop=True)
                else:
                    q = job - F_ACC
                    for d in range(KD):
                        nc.tensor.matmul(front_bank, xnT[:, d, q * P:(q + 1) * P], w_in_sb[:, d, DI:2 * DI], start=(d == 0), stop=False)
                    for e in range(ET):
                        last = nc.tensor.matmul(front_bank[:, e * P:(e + 1) * P], xc[:, e, q * P:(q + 1) * P], d_diag[:, e],
                                                start=False, stop=(e == ET - 1))
                last.then_inc(front_full, 1)

            def post(c, par, n):
                job = PE_POST.get(n)
                if job is None:
                    return
                pe.wait_ge(post_taken, post_job(c, job))
                if job < 2:
                    pe.wait_ge(g_ready, c + 1)
                    for i in range(2):
                        e = 2 * job + i
                        for q in range(NT):
                            last = nc.tensor.transpose(post_bank[:, i * T + q * P:i * T + (q + 1) * P], g[:, q, e * P:(e + 1) * P], ident[:])
                else:
                    for q in range(NT):
                        for e in range(ET):
                            last = nc.tensor.matmul(post_bank[:, q * DIM:(q + 1) * DIM], gT[:, e, q * P:(q + 1) * P], w_out_sb[:, e],
                                                    start=(e == 0), stop=(e == ET - 1))
                last.then_inc(post_full, 1)

            def pair_rows(c, par, k):
                after(pe, post_taken, pair_job(c, k))
                for j in range(2):
                    last = nc.tensor.matmul(post_bank[:, j * T:(j + 1) * T], select(ROW_B + 2 * k + j), ssm[:, par], start=True, stop=True)
                last.then_inc(post_full, 1)

            def scan(c, par, between, more):
                for n in range(NS):
                    pe.wait_ge(scan_done, NS * c + n + 1)
                    for q in range(NT):
                        after(pe, y_added[q], NS * c + n)
                        for e in range(ET):
                            last = nc.tensor.transpose(turned[q][:, e * P:(e + 1) * P], h[:, n % 2, e, q * P:(q + 1) * P], ident[:])
                        last.then_inc(turn_full[q], 1)
                    between(n)
                    if n % 2 == 0:
                        k = n // 2 + 2
                        if k < PAIRS:
                            pair_rows(c, par, k)
                        elif more:
                            pair_rows(c + 1, 1 - par, k - PAIRS)

            def start():
                pair_rows(0, 0, 0)
                pair_rows(0, 0, 1)

            bodies(front, scan, post, start, pe)

            pe.wait_ge(flag_step, FLAG_STEPS)
            last = nc.tensor.matmul(ring[0][0:1, 0:1], not_exact[:], ones[:], start=True, stop=True)
            last.then_inc(count_ready, 1)

            pe.wait_ge(mlp_weights_in, 16 * 10)

            def free(job):
                bank, place, of_bank = job
                after(pe, ring_taken[bank], of_bank)
                return ring[bank]

            def turn_rows(c):
                pe.wait_ge(xn_b_ready, c + 1)
                for d in range(KD):
                    bank = free(turn_job(c, d))
                    for q in range(NTB):
                        last = nc.tensor.transpose(bank[:, q * P:(q + 1) * P], xn_b[:, q, d * P:(d + 1) * P], ident[:])
                    last.then_inc(ring_full, 1)

            def pass_b(exact):
                def weights_of(name):
                    return rounded[name] if exact else full[name]

                def parts_of(name):
                    return (high[name], low[name]) if exact else (whole[name],)

                def wait_row(c, k, first_split, rows_ready):
                    if exact:
                        pe.wait_ge(rows_split, split_job(c, first_split + k) + 1)
                    else:
                        pe.wait_ge(rows_ready, KH * c + k + 1)

                def layer(c, job0, weights, rows, first_split, rows_ready):
                    first = RING // 2
                    tiles = [list(range(first))] + [[o] for o in range(first, KH)]
                    parts = parts_of(rows)
                    for group in tiles:
                        banks_of = [free(ring_job(c, job0 + o)) for o in group]
                        for k in range(KH):
                            if group[0] == 0:
                                wait_row(c, k, first_split, rows_ready)
                            for o, bank in zip(group, banks_of):
                                for i, part in enumerate(parts):
                                    last = nc.tensor.matmul(bank, weights[:, k, o * P:(o + 1) * P], part[:, k],
                                                            start=(k + i == 0), stop=(k == KH - 1 and i == len(parts) - 1))
                                if k == KH - 1:
                                    last.then_inc(ring_full, 1)

                def body(c, par, more):
                    if exact:
                        pe.wait_ge(rows_split, split_turn(c, KD - 1) + 1)
                    else:
                        pe.wait_ge(xnT_b_ready, KD * (c + 1))
                    parts = parts_of("xnT_b")
                    for o in range(KH):
                        for j, weights in enumerate((weights_of("w1"), weights_of("w2"))):
                            bank = free(ring_job(c, J_L1 + 2 * o + j))
                            for d in range(KD):
                                for i, part in enumerate(parts):
                                    last = nc.tensor.matmul(bank, weights[:, d, o * P:(o + 1) * P], part[:, d],
                                                            start=(d + i == 0), stop=(d == KD - 1 and i == len(parts) - 1))
                            last.then_inc(ring_full, 1)
                    layer(c, J_H1, weights_of("h1"), "act1", 0, gated_ready)
                    if more:
                        turn_rows(c + 1)
                    if exact and isinstance(c, int) and c == 0:
                        pe.wait_ge(rounded_pool, 1)
                        pe.wait_ge(rounded_act, 1)
                    layer(c, J_H2, weights_of("h2"), "act2", S_H1, hidden1_ready)
                    banks_of = [free(ring_job(c, J_OUT + j)) for j in range(NTB // 2)]
                    parts = parts_of("act1")
                    w3_of = weights_of("w3")
                    for half in range(2):
                        for k in range(KH):
                            if half == 0:
                                wait_row(c, k, S_H2, hidden2_ready)
                            for j, bank in enumerate(banks_of):
                                q = 2 * j + half
                                for i, part in enumerate(parts):
                                    last = nc.tensor.matmul(bank[:, half * DIM:(half + 1) * DIM], part[:, k, q * P:(q + 1) * P], w3_of[:, k],
                                                            start=(k + i == 0), stop=(k == KH - 1 and i == len(parts) - 1))
                                if half == 1 and k == KH - 1:
                                    last.then_inc(ring_full, 1)

                turn_rows(0)
                if exact:
                    pe.wait_ge(rounded_dve, 3)
                bodies_b(pe, body)

            on_flag(pe, pass_b)


_INS = ["x", "w_in", "conv_w", "conv_b", "w_x", "w_dt", "b_dt", "a_log", "d_skip", "w_out",
        "w1", "s1", "w2", "s2", "h1", "t1", "h2", "t2", "w3", "s3"]


def kernel(**inputs):
    import numpy as np
    import concourse.bacc as bacc
    from concourse.bass_utils import run_bass_kernel_spmd

    a = {k[3:]: np.asarray(v) for k, v in inputs.items()}

    def turn(w):
        return np.ascontiguousarray(w.T)

    def columns(v):
        return np.ascontiguousarray(v.reshape(-1, P).T)

    arrays = {
        "x": a["attn_x"], "w_in": turn(a["attn_W_in"]), "conv_w": a["attn_conv_w"], "conv_b": columns(a["attn_conv_b"]),
        "w_x": turn(a["attn_W_x"]), "w_dt": columns(a["attn_W_dt"]), "b_dt": columns(a["attn_b_dt"]),
        "a_log": a["attn_A_log"], "d_skip": columns(a["attn_D"]), "w_out": turn(a["attn_W_out"]),
        "w1": turn(a["ffn_w1_w"]), "s1": columns(a["ffn_w1_s"]), "w2": turn(a["ffn_w2_w"]), "s2": columns(a["ffn_w2_s"]),
        "h1": turn(a["ffn_h1_w"]), "t1": columns(a["ffn_h1_s"]), "h2": turn(a["ffn_h2_w"]), "t2": columns(a["ffn_h2_s"]),
        "w3": turn(a["ffn_w3_w"]), "s3": a["ffn_w3_s"],
    }
    nc = bacc.Bacc("TRN2", target_bir_lowering=False, num_devices=1)
    args = [nc.dram_tensor(f"in_{k}", arrays[k].shape, mybir.dt.from_np(arrays[k].dtype), kind="ExternalInput").ap() for k in _INS]
    x1 = nc.dram_tensor("x1_scratch", arrays["x"].shape, F32, kind="Internal").ap()
    out = nc.dram_tensor("out", arrays["x"].shape, F32, kind="ExternalOutput").ap()
    program(nc, *args, x1, out)
    r = run_bass_kernel_spmd(nc, [{f"in_{k}": arrays[k] for k in _INS}], core_ids=[0])
    return r.results[0]["out"]
```

```python
from contextlib import ExitStack

import concourse.bass as bass
from concourse import mybir

F32 = mybir.dt.float32
F32R = mybir.dt.float32r
I32 = mybir.dt.int32
ALU = mybir.AluOpType
ACT = mybir.ActivationFunctionType

P = 128
EPS = 1e-5
LOW = -40.0
HIGH = 40.0
T = 256
NT = T // P
TB = 512
NTB = TB // P


def program(nc, x, w_in, conv_w, conv_b, w_x, w_dt, b_dt, a_log, d_skip, w_out,
            w1, s1, w2, s2, h1, t1, h2, t2, w3, s3, x1_dram, out):
    BATCH, SEQ, DIM = x.shape
    DI = w_out.shape[0]
    TAPS = conv_w.shape[-1]
    NS = a_log.shape[0]
    HID = w1.shape[1]
    KD, ET, KH = DIM // P, DI // P, HID // P
    CHUNKS = BATCH * SEQ // T
    PER_SEQ = SEQ // T
    CB = BATCH * SEQ // TB
    HALO = TAPS - 1
    PIECE = NT * DI
    LOW_MASK = 0xFFF
    FLAG_STEPS = (2 * KD + 2 * KH + KH * DIM // HID) * HID // PIECE + 3
    ROW_B, ROW_C, ROW_DT = 0, 32, 64
    assert DIM == 2 * P and DI == 4 * P and NT == 2 and NS % 2 == 0 and CHUNKS % 2 == 0 and CHUNKS >= 4

    x_rows = x.rearrange("b (c n p) d -> p (b c) n d", p=P, n=NT)
    x1_rows = x1_dram.rearrange("b (c n p) d -> p (b c) n d", p=P, n=NT)
    x1_rows_b = x1_dram.rearrange("b (c n p) d -> p (b c) n d", p=P, n=NTB)
    out_rows = out.rearrange("b (c n p) d -> p (b c) n d", p=P, n=NTB)

    with ExitStack() as ctx:
        def sb(name, shape, dt=F32, where=ctx):
            return where.enter_context(nc.sbuf_tensor(name, shape, dt))

        def sem(name):
            return ctx.enter_context(nc.semaphore(name))

        ident = sb("ident", [P, P])
        eps = sb("eps", [P, 1])
        mlp_shapes = {"w1": [P, KD, HID], "w2": [P, KD, HID], "h1": [P, KH, HID], "h2": [P, KH, HID], "w3": [P, KH, DIM]}
        with ExitStack() as as_loaded:
            full = {name: sb(f"{name}_full", shape, where=as_loaded) for name, shape in mlp_shapes.items()}
        rounded = {name: sb(f"{name}_rounded", shape, F32R) for name, shape in mlp_shapes.items()}
        flag = sb("flag", [1, 1], I32)
        scales = sb("scales", [P, 4, KH])
        s3_row = sb("s3_row", [P, DIM])

        a_only = ctx.enter_context(ExitStack())
        w_in_sb = sb("w_in_sb", [P, KD, 2 * DI], where=a_only)
        w_x_sb = sb("w_x_sb", [P, ET, P], where=a_only)
        conv_diag = sb("conv_diag", [P, ET, TAPS, P], where=a_only)
        d_diag = sb("d_diag", [P, ET, P], where=a_only)
        x_sb = sb("x_sb", [P, 2, NT, DIM], where=a_only)
        xn = sb("xn", [P, NT, DIM], where=a_only)
        xnT = sb("xnT", [P, KD, T], where=a_only)
        xp = sb("xp", [P, ET, HALO + T], where=a_only)
        w_out_sb = sb("w_out_sb", [P, ET, DIM], where=a_only)
        conv_w_sb = sb("conv_w_sb", [P, ET, TAPS], where=a_only)
        conv_b_sb = sb("conv_b_sb", [P, ET], where=a_only)
        w_dt_sb = sb("w_dt_sb", [P, ET], where=a_only)
        b_dt_sb = sb("b_dt_sb", [P, ET], where=a_only)
        d_sb = sb("d_sb", [P, ET], where=a_only)
        neg_a = sb("neg_a", [P, NS], where=a_only)
        keep = sb("keep", [P, CHUNKS + 1], where=a_only)
        keep_next = sb("keep_next", [P, 2], where=a_only)
        bn = sb("bn", [P, NT, 6], where=a_only)
        mv = sb("mv", [P, NT, 2], where=a_only)
        log_var = sb("log_var", [P, NT], where=a_only)
        rstd = sb("rstd", [P, NT], where=a_only)
        sig = sb("sig", [P, ET, T], where=a_only)
        xc = sb("xc", [P, ET, T], where=a_only)
        ssm = sb("ssm", [P, 2, T], where=a_only)
        c_tok = sb("c_tok", [P, 2, NT, NS], where=a_only)
        dt = sb("dt", [P, 2, ET, T], where=a_only)
        u = sb("u", [P, 2, ET, T], where=a_only)
        b_row = sb("b_row", [P, 2, 2, T], where=a_only)
        ub = sb("ub", [P, 2, ET, 1 + T], where=a_only)
        decay = sb("decay", [P, 2, ET, 1 + T], where=a_only)
        h = sb("h", [P, 2, ET, 1 + T], where=a_only)
        one = sb("one", [P, 1], where=a_only)
        carry = sb("carry", [P, NS, ET], where=a_only)
        acc = sb("acc", [P, 2, NT, DI], where=a_only)
        gsig = sb("gsig", [P, NT, DI], where=a_only)
        g = sb("g", [P, NT, DI], where=a_only)
        gT = gsig[:].rearrange("p n d -> p (n d)").rearrange("p (e t) -> p e t", t=T)
        z = g[:].rearrange("p n d -> p (n d)").rearrange("p (e t) -> p e t", t=T)
        soft = sig
        low_bits = gsig[:].rearrange("p n d -> p (n d)").bitcast(I32)
        x_res = sb("x_res", [P, 2, NT, DIM], where=a_only)
        x1_sb = sb("x1_sb", [P, 2, NT, DIM], where=a_only)
        low_found = sb("low_found", [P, 1], I32, where=a_only)
        not_exact = sb("not_exact", [P, 1], where=a_only)
        ones = sb("ones", [P, 1], where=a_only)
        a_only.close()

        xb = sb("xb", [P, 2, NTB, DIM])
        bn_b = sb("bn_b", [P, NTB, 6])
        mv_b = sb("mv_b", [P, NTB, 2])
        log_var_b = sb("log_var_b", [P, NTB])
        rstd_b = sb("rstd_b", [P, NTB])
        xn_b = sb("xn_b", [P, NTB, DIM])
        WIDE = 4
        wide = sb("wide", [P, WIDE, TB])
        row_shapes = {"xnT_b": [P, KD, TB], "act1": [P, KH, TB], "act2": [P, KH, TB]}
        with ExitStack() as whole_only:
            whole = {name: sb(f"{name}_whole", shape, where=whole_only) for name, shape in row_shapes.items()}
        high, low = {}, {}
        for name, shape in row_shapes.items():
            high[name] = sb(f"{name}_high", shape, F32R)
            low[name] = sb(f"{name}_low", shape, F32R)
        silu_b = sb("silu_b", [P, 2, TB])
        prod_b = sb("prod_b", [P, NTB, DIM])
        out_sb = sb("out_sb", [P, 2, NTB, DIM])

        banks = ctx.enter_context(nc.psum_tensor("banks", [P, 8, 512], F32))
        turned = [[banks[:, NT * s + n, :] for n in range(NT)] for s in range(2)]
        front_banks = [banks[:, 4 + n, :] for n in range(2)]
        post_bank = banks[:, 6, :]
        pair_bank = banks[:, 7, :]
        ring = [banks[:, (4 + n) % 8, :] for n in range(6)]

        weights_in = sem("weights_in")
        mlp_weights_in = sem("mlp_weights_in")
        setup = sem("setup")
        a_ready = sem("a_ready")
        diag_ready = sem("diag_ready")
        x_in = sem("x_in")
        bn_done = sem("bn_done")
        stats_ready = sem("stats_ready")
        logvar_done = sem("logvar_done")
        rstd_ready = sem("rstd_ready")
        xn_ready = sem("xn_ready")
        front_full = sem("front_full")
        front_taken = {eng: sem(f"front_taken_{eng}") for eng in ("act", "dve")}
        halo_ready = sem("halo_ready")
        silu_step = sem("silu_step")
        xc_ready = sem("xc_ready")
        zmin_ready = sem("zmin_ready")
        soft_step = sem("soft_step")
        dt_ready = sem("dt_ready")
        u_ready = sem("u_ready")
        decay_ready = sem("decay_ready")
        ub_ready = sem("ub_ready")
        scan_done = sem("scan_done")
        carry_ready = sem("carry_ready")
        keep_ready = sem("keep_ready")
        turn_full = [sem(f"turn_full{n}") for n in range(NT)]
        y_added = [sem(f"y_added{n}") for n in range(NT)]
        pair_full = sem("pair_full")
        pair_taken = sem("pair_taken")
        gm_ready = sem("gm_ready")
        gate_step = sem("gate_step")
        g_ready = sem("g_ready")
        g_turned = sem("g_turned")
        gT_ready = sem("gT_ready")
        y_out_full = sem("y_out_full")
        xres_in = sem("xres_in")
        x1_ready = sem("x1_ready")
        x1_out = sem("x1_out")

        def after(eng, s, value):
            if not (isinstance(value, int) and value <= 0):
                eng.wait_ge(s, value)

        FJ = 10
        F_XN, F_XP, F_CONV, F_SSM, F_DT, F_C, F_ACC = 0, 1, 3, 5, 6, 7, 8
        TAKER = {k: "dve" if k in (F_CONV, F_CONV + 1) else "act" for k in range(FJ)}
        DVE_AT = dict(stats=6, normalize=11, conv=(3, 4), silu=6, z=10, dt=11, gate_low=0, gate=5, x1=14)
        ACT_AT = dict(rstd=12, xn=0, xp=(2, 3), silu=8, ssm=11, soft=13, c=12, acc=(14, 15), gate=5, gT=(9, 11), z=12)
        PE_AT = dict(xn=13, next_xp=15, xp=0, conv=((1, 2), (3, 4)), ssm=8, dt=9, c=9, acc=(10, 11), gT=(6, 7), out=(12, 14))
        POOL_AT = dict(u=15)
        B_FIRST = dict(stats=3, rstd=8, normalize=7, turn=10)
        PAIRS = NS // 2

        def first_norm(c):
            return isinstance(c, int) and c < 2

        def last_body(c):
            return isinstance(c, int) and c == CHUNKS - 1

        def front_bank(k):
            return front_banks[k % 2]

        def front_job(c, k):
            return FJ * c + k

        def wait_taken(eng, c, k):
            c, k = c + k // FJ, k % FJ
            taker = TAKER[k]
            before = sum(TAKER[i] == taker for i in range(k))
            each = sum(t == taker for t in TAKER.values())
            after(eng, front_taken[taker], each * c + before + 1 if not (isinstance(c, int) and c < 0) else 0)

        def bodies(norm, front, scan, post, start, eng):
            def body(c, par, has_norm, has_front, has_post):
                def between(n):
                    if has_post:
                        post(c - 1, 1 - par, n)
                    if has_front:
                        front(c + 1, 1 - par, n)
                    if has_norm:
                        norm(c + 2, par, n)
                scan(c, par, between, has_front)

            for n in range(NS):
                norm(0, 0, n)
            for n in range(NS):
                front(0, 0, n)
            start()
            for n in range(NS):
                norm(1, 1, n)
            body(0, 0, True, True, False)
            body(1, 1, True, True, True)
            with eng.Fori(1, CHUNKS // 2 - 1) as pair:
                body(2 * pair, 0, True, True, True)
                body(2 * pair + 1, 1, True, True, True)
            body(CHUNKS - 2, 0, False, True, True)
            body(CHUNKS - 1, 1, False, False, True)
            for n in range(NS):
                post(CHUNKS - 1, 1, n)

        def sigmoid(dst, src, ready, value, step, base, act):
            after(act, ready, value)
            nc.scalar.activation(dst, src, ACT.Exp, scale=-1.0).then_inc(step, 1)
            act.wait_ge(step, base + 1)
            nc.scalar.activation(dst, dst, ACT.Ln, bias=1.0).then_inc(step, 1)
            act.wait_ge(step, base + 2)
            nc.scalar.activation(dst, dst, ACT.Exp, scale=-1.0).then_inc(step, 1)

        RING = 6
        J_L1, J_H1 = 0, 2 * KH
        J_T = J_H1 + KH
        J_H2 = J_T + KD
        J_OUT = J_H2 + KH
        BJOBS = J_OUT + NTB // 2
        assert BJOBS % RING == 0
        xb_in = sem("xb_in")
        bn_b_done = sem("bn_b_done")
        stats_b_ready = sem("stats_b_ready")
        logvar_b_done = sem("logvar_b_done")
        rstd_b_ready = sem("rstd_b_ready")
        xn_b_ready = sem("xn_b_ready")
        ring_full = sem("ring_full")
        ring_taken = [sem(f"ring_taken{n}") for n in range(RING)]
        xnT_b_ready = sem("xnT_b_ready")
        silu_b_ready = sem("silu_b_ready")
        gated_ready = sem("gated_ready")
        hidden1_ready = sem("hidden1_ready")
        hidden2_ready = sem("hidden2_ready")
        prod_ready = sem("prod_ready")
        out_ready = sem("out_ready")
        out_stored = sem("out_stored")

        wide_ready = sem("wide_ready")
        high_ready = sem("high_ready")
        rows_split = sem("rows_split")
        flag_step = sem("flag_step")
        count_ready = sem("count_ready")
        flag_ready = sem("flag_ready")
        rounded_dve = sem("rounded_dve")
        rounded_pool = sem("rounded_pool")
        rounded_act = sem("rounded_act")

        S_H1, S_T, S_H2 = KH, 2 * KH, 2 * KH + KD
        SJOBS = 3 * KH + KD
        assert 2 * SJOBS % WIDE == 0 and (KD + SJOBS * -1 + S_T) % WIDE == 0

        def split_job(c, k):
            if isinstance(c, int) and c == CB - 1 and k >= S_H2:
                k -= KD
            return KD + SJOBS * c + k

        def split_turn(c, d):
            return d if isinstance(c, int) and c == 0 else split_job(c - 1, S_T + d)

        def wide_slot(par, k):
            return (KD + SJOBS * par + k) % WIDE

        def wide_turn_slot(par, d):
            return wide_slot(1 - par, S_T + d)

        def pass_a_over(eng):
            eng.wait_ge(x1_out, 16 * CHUNKS)
            eng.wait_ge(carry_ready, NS * CHUNKS)

        def on_flag(eng, pass_b):
            eng.wait_ge(flag_ready, 1)
            value = eng.value_load(flag[0:1, 0:1])
            with eng.If(value == 0):
                pass_b(True)
            with eng.Else():
                pass_b(False)

        def ring_job(c, k):
            if isinstance(c, int) and c == CB - 1 and k >= J_H2:
                k -= KD
            return (KD + k) % RING, KD + BJOBS * c + k, BJOBS // RING * c + (KD + k) // RING

        def turn_job(c, d):
            return (d % RING, d, 0) if isinstance(c, int) and c == 0 else ring_job(c - 1, J_T + d)

        def bodies_b(eng, body):
            body(0, 0, True)
            body(1, 1, True)
            with eng.Fori(1, CB // 2 - 1) as pair:
                body(2 * pair, 0, True)
                body(2 * pair + 1, 1, True)
            body(CB - 2, 0, True)
            body(CB - 1, 1, False)

        block = ctx.enter_context(nc.Block())

        @block.sync
        def _(sp):
            sp.dma_start(w_in_sb[:], w_in.rearrange("(k p) n -> p k n", p=P)).then_inc(weights_in, 16)
            sp.dma_start(conv_w_sb[:], conv_w.rearrange("(e p) o k -> p e (o k)", p=P)).then_inc(weights_in, 16)
            for dst, src in ((conv_b_sb, conv_b), (w_dt_sb, w_dt), (b_dt_sb, b_dt), (d_sb, d_skip)):
                sp.dma_start(dst[:], src).then_inc(weights_in, 16)
            sp.dma_start(neg_a[:], a_log.rearrange("(o n) -> o n", o=1).to_broadcast([P, NS])).then_inc(weights_in, 16)
            sp.dma_start(w_out_sb[:], w_out.rearrange("(k p) n -> p k n", p=P)).then_inc(weights_in, 16)
            sp.wait_ge(setup, 8)
            w_x_rows = w_x.rearrange("(k p) n -> p k n", p=P)
            sp.dma_start(w_x_sb[:, :, ROW_B:ROW_B + NS], w_x_rows[:, :, 0:NS]).then_inc(weights_in, 16)
            sp.dma_start(w_x_sb[:, :, ROW_C:ROW_C + NS], w_x_rows[:, :, NS:2 * NS]).then_inc(weights_in, 16)
            with nc.allow_non_contiguous_dma(reason="the one column of dt, once"):
                sp.dma_start(w_x_sb[:, :, ROW_DT:ROW_DT + 1], w_x_rows[:, :, 2 * NS:]).then_inc(weights_in, 16)

            def both(first, first_value, second, second_value):
                values = [v if isinstance(v, int) else sp.snap(v) for v in (first_value, second_value)]
                sp.wait_ge(setup, 8)
                after(sp, first, values[0])
                after(sp, second, values[1])

            def load_x(c, par):
                both(xn_ready, c - 1, x_in, 16 * c)
                sp.dma_start(x_sb[:, par:par + 1], x_rows[:, bass.ds(c, 1)]).then_inc(x_in, 16)

            def load_res(c, par):
                both(x1_ready, c - 1, xres_in, 16 * c)
                sp.dma_start(x_res[:, par:par + 1], x_rows[:, bass.ds(c, 1)]).then_inc(xres_in, 16)

            def store_x1(c, par):
                both(x1_ready, c + 1, x1_out, 16 * c)
                sp.dma_start(x1_rows[:, bass.ds(c, 1)], x1_sb[:, par:par + 1]).then_inc(x1_out, 16)

            load_x(0, 0)
            load_x(1, 1)
            load_res(0, 0)
            load_res(1, 1)
            for dst, src in ((full["w1"], w1), (full["w2"], w2), (full["h1"], h1), (full["h2"], h2), (full["w3"], w3)):
                sp.dma_start(dst[:], src.rearrange("(k p) n -> p k n", p=P)).then_inc(mlp_weights_in, 16)
            for k, s in enumerate((s1, s2, t1, t2)):
                sp.dma_start(scales[:, k], s).then_inc(mlp_weights_in, 16)
            sp.dma_start(s3_row[:], s3.rearrange("(o n) -> o n", o=1).to_broadcast([P, DIM])).then_inc(mlp_weights_in, 16)
            load_x(2, 0)
            load_x(3, 1)
            with sp.Fori(1, CHUNKS // 2 - 1) as pair:
                for k in range(2):
                    c = 2 * pair + k
                    load_x(c + 2, k)
                    store_x1(c - 2, k)
                    load_res(c, k)
            for c in (CHUNKS - 2, CHUNKS - 1):
                store_x1(c - 2, c % 2)
                load_res(c, c % 2)

            def load_b(c, par):
                both(out_ready, c - 1, xb_in, 16 * c)
                sp.dma_start(xb[:, par:par + 1], x1_rows_b[:, bass.ds(c, 1)]).then_inc(xb_in, 16)

            sp.wait_ge(front_full, FJ * CHUNKS)
            sp.wait_ge(x1_out, 16 * (TB // T))
            load_b(0, 0)
            for c in (CHUNKS - 2, CHUNKS - 1):
                store_x1(c, c % 2)
            pass_a_over(sp)

            def body(c, par, more):
                if more:
                    load_b(c + 1, 1 - par)
                both(out_ready, c + 1, out_stored, 16 * c)
                sp.dma_start(out_rows[:, bass.ds(c, 1)], out_sb[:, par:par + 1]).then_inc(out_stored, 16)

            def pass_b(exact):
                bodies_b(sp, body)
                sp.wait_ge(out_stored, 16 * CB)

            on_flag(sp, pass_b)

        @block.gpsimd
        def _(pool):
            nc.gpsimd.memset(w_x_sb[:], 0.0).then_inc(setup, 1)
            nc.gpsimd.memset(ident[:], 1.0).then_inc(setup, 1)
            nc.gpsimd.memset(eps[:], EPS).then_inc(setup, 1)
            nc.gpsimd.memset(keep[:], 1.0).then_inc(setup, 1)
            nc.gpsimd.memset(carry[:], 0.0).then_inc(setup, 1)
            nc.gpsimd.memset(xp[:], 0.0).then_inc(setup, 1)
            nc.gpsimd.memset(decay[:, :, :, 0:1], 0.0).then_inc(setup, 1)
            nc.gpsimd.memset(one[:], 1.0).then_inc(setup, 1)
            pool.wait_ge(setup, 8)
            nc.gpsimd.affine_select(out=ident[:], in_=ident[:], compare_op=ALU.is_equal, fill=0.0, base=0,
                                    pattern=[[-1, P]], channel_multiplier=1).then_inc(setup, 1)
            nc.gpsimd.memset(keep[:, 0:CHUNKS:PER_SEQ], 0.0).then_inc(setup, 1)
            pool.wait_ge(setup, 10)

            def front(c, par, n):
                if n == POOL_AT["u"]:
                    pool.wait_ge(dt_ready, c + 1)
                    nc.gpsimd.tensor_tensor(u[:, par], dt[:, par], xc[:], ALU.mult).then_inc(u_ready, 1)

            def scan(c, par, between, more):
                pool.wait_ge(u_ready, c + 1)
                pool.wait_ge(keep_ready, c + 1)

                def carry_out(n):
                    pool.wait_ge(scan_done, NS * c + n + 1)
                    nc.gpsimd.tensor_tensor(carry[:, n, :], h[:, n % 2, :, T],
                                            keep_next[:, par:par + 1].to_broadcast([P, ET]), ALU.mult).then_inc(carry_ready, 1)

                for n in range(NS):
                    if n % 2 == 0:
                        pool.wait_ge(pair_taken, PAIRS * c + n // 2 + 1)
                    after(pool, scan_done, NS * c + n - 1)
                    after(pool, carry_ready, NS * (c - 1) + n + 1)
                    nc.gpsimd.tensor_tensor(ub[:, n % 2, :, 0], carry[:, n, :], one[:].to_broadcast([P, ET]), ALU.mult)
                    nc.gpsimd.tensor_tensor(ub[:, n % 2, :, 1:], u[:, par],
                                            b_row[:, (n // 2) % 2, n % 2:n % 2 + 1, :].to_broadcast([P, ET, T]),
                                            ALU.mult).then_inc(ub_ready, 1)
                    if n >= 1:
                        carry_out(n - 1)
                    between(n)
                carry_out(NS - 1)

            bodies(lambda c, par, n: None, front, scan, lambda c, par, n: None, lambda: None, pool)

            pool.wait_ge(mlp_weights_in, 16 * 10)

            def pass_b(exact):
                if exact:
                    for name in ("h2", "w3"):
                        nc.gpsimd.tensor_copy(rounded[name][:], full[name][:]).then_inc(rounded_pool, 1)

            on_flag(pool, pass_b)

        @block.scalar
        def _(act):
            nc.scalar.preload_act_table_set("natural_log_exp_and_others")
            act.wait_ge(weights_in, 16 * 11)
            nc.scalar.activation(neg_a[:], neg_a[:], ACT.Exp).then_inc(a_ready, 1)
            act.wait_ge(diag_ready, 1)
            act.wait_ge(setup, 10)

            def after_setup(s, value):
                value = value if isinstance(value, int) else act.snap(value)
                act.wait_ge(setup, 10)
                after(act, s, value)

            def take_front(c, k, dst, src):
                act.wait_ge(front_full, front_job(c, k) + 1)
                nc.scalar.activation(dst, src, ACT.Copy).then_inc(front_taken["act"], 1)

            def take_acc(c, par, q):
                after(act, gm_ready, c - 1)
                take_front(c, F_ACC + q, acc[:, par, q], front_bank(F_ACC + q))

            def take_pair(c, k):
                act.wait_ge(pair_full, PAIRS * c + k + 1)
                after(act, ub_ready, NS * c + 2 * k - 2)
                nc.scalar.activation(b_row[:, k % 2], pair_bank.rearrange("p (n t) -> p n t", n=2), ACT.Copy).then_inc(pair_taken, 1)

            def norm(c, par, n):
                if n == ACT_AT["rstd"]:
                    act.wait_ge(stats_ready, c + 1)
                    nc.scalar.activation(log_var[:], mv[:, :, 1], ACT.Ln, bias=eps[:, 0:1]).then_inc(logvar_done, 1)
                    act.wait_ge(logvar_done, c + 1)
                    nc.scalar.activation(rstd[:], log_var[:], ACT.Exp, scale=-0.5).then_inc(rstd_ready, 1)

            def front(c, par, n):
                if n == ACT_AT["xn"]:
                    take_front(c, F_XN, xnT[:].rearrange("p k t -> p (k t)"), front_bank(F_XN))
                if n == ACT_AT["xp"][0]:
                    act.wait_ge(front_full, front_job(c, F_XP) + 1)
                    goes_on = keep[:, 0:1] if isinstance(c, int) and c == 0 else keep_next[:, 1 - par:2 - par]
                    after(act, keep_ready, c)
                    nc.scalar.activation(xp[:, :, 0:HALO], xp[:, :, T:T + HALO], ACT.Copy,
                                         scale=goes_on).then_inc(halo_ready, 1)
                    act.wait_ge(halo_ready, c + 1)
                if n in ACT_AT["xp"]:
                    j = ACT_AT["xp"].index(n)
                    take_front(c, F_XP + j, xp[:, 2 * j:2 * j + 2, HALO:], front_bank(F_XP + j).rearrange("p (e t) -> p e t", e=2))
                if n == ACT_AT["silu"]:
                    sigmoid(sig[:], xc[:], front_taken["dve"], 2 * (c + 1), silu_step, 3 * c, act)
                if n == ACT_AT["ssm"]:
                    take_front(c, F_SSM, ssm[:, par], front_bank(F_SSM)[:, 0:T])
                if n == ACT_AT["z"]:
                    after(act, g_turned, 2 * (c - 1))
                    act.wait_ge(front_full, front_job(c, F_DT) + 1)
                    for e in range(ET):
                        last = nc.scalar.activation(z[:, e], front_bank(F_DT)[:, 0:T], ACT.Identity, scale=w_dt_sb[:, e:e + 1], bias=b_dt_sb[:, e:e + 1])
                    last.then_inc(front_taken["act"], 1)
                if n == ACT_AT["soft"]:
                    act.wait_ge(zmin_ready, c + 1)
                    nc.scalar.activation(soft[:], soft[:], ACT.Exp).then_inc(soft_step, 1)
                    act.wait_ge(soft_step, 2 * c + 1)
                    nc.scalar.activation(soft[:], soft[:], ACT.Ln, bias=1.0).then_inc(soft_step, 1)
                if n == ACT_AT["c"]:
                    take_front(c, F_C, c_tok[:, par], front_bank(F_C)[:, 0:NT * P].rearrange("p (n r) -> p n r", n=NT)[:, :, ROW_C:ROW_C + NS])
                if n in ACT_AT["acc"]:
                    take_acc(c, par, ACT_AT["acc"].index(n))
                if n == 15:
                    take_pair(c, 0)

            def post(c, par, n):
                if n == ACT_AT["gate"]:
                    sigmoid(gsig[:], g[:], gm_ready, c + 1, gate_step, 3 * c, act)
                if n in ACT_AT["gT"]:
                    j = ACT_AT["gT"].index(n)
                    act.wait_ge(g_turned, 2 * c + j + 1)
                    nc.scalar.activation(gT[:, 2 * j:2 * j + 2], post_bank.rearrange("p (e t) -> p e t", e=2), ACT.Copy).then_inc(gT_ready, 1)

            def rstd_of(c):
                act.wait_ge(stats_b_ready, c + 1)
                nc.scalar.activation(log_var_b[:], mv_b[:, :, 1], ACT.Ln, bias=eps[:, 0:1]).then_inc(logvar_b_done, 1)
                act.wait_ge(logvar_b_done, c + 1)
                nc.scalar.activation(rstd_b[:], log_var_b[:], ACT.Exp, scale=-0.5).then_inc(rstd_b_ready, 1)

            def scan(c, par, between, more):
                act.wait_ge(dt_ready, c + 1)
                after_setup(carry_ready, NS * (c - 1))
                nc.scalar.activation(keep_next[:, par:par + 1], keep[:, bass.ds(c + 1, 1)], ACT.Copy).then_inc(keep_ready, 1)
                for n in range(NS):
                    if n % 2 == 1:
                        take_pair(c, (n + 1) // 2) if n < NS - 1 else None
                    after(act, scan_done, NS * c + n - 1)
                    nc.scalar.activation(decay[:, n % 2, :, 1:], dt[:, par], ACT.Exp, scale=neg_a[:, n:n + 1]).then_inc(decay_ready, 1)
                    between(n)
                    if last_body(c) and n == B_FIRST["rstd"]:
                        rstd_of(0)

            bodies(norm, front, scan, post, lambda: None, act)

            act.wait_ge(mlp_weights_in, 16 * 10)

            def take(job, dst, func, scale, done):
                bank, place, of_bank = job
                act.wait_ge(ring_full, place + 1)
                nc.scalar.activation(dst, ring[bank], func, scale=scale).then_inc(ring_taken[bank], 1)
                act.wait_ge(ring_taken[bank], of_bank + 1)
                act.sem_inc(done, 1)

            def take_wide(job, row, slot, func, scale):
                after(act, rows_split, row - WIDE + 1)
                take(job, wide[:, slot], func, scale, wide_ready)

            def turned_rows(c, par, exact):
                for d in range(KD):
                    if exact:
                        take_wide(turn_job(c, d), split_turn(c, d), wide_turn_slot(par, d), ACT.Copy, 1.0)
                    else:
                        take(turn_job(c, d), whole["xnT_b"][:, d], ACT.Copy, 1.0, xnT_b_ready)

            def high_gated(c, par, o):
                row = split_job(c, o)
                act.wait_ge(wide_ready, row + 1)
                nc.scalar.activation(high["act1"][:, o], wide[:, wide_slot(par, o)], ACT.Copy).then_inc(high_ready, 1)

            def pass_b(exact):
                def body(c, par, more):
                    for o in range(KH):
                        if not exact:
                            after(act, gated_ready, KH * c + o - 1)
                        elif o >= 2:
                            act.wait_ge(wide_ready, split_job(c, o - 2) + 1)
                        take(ring_job(c, J_L1 + 2 * o), silu_b[:, o % 2], ACT.Silu, scales[:, 0, o:o + 1], silu_b_ready)
                        if exact and o >= 1:
                            high_gated(c, par, o - 1)
                    if exact:
                        high_gated(c, par, KH - 1)
                    for o in range(KH):
                        if more and o == 2:
                            rstd_of(c + 1)
                        if exact:
                            take_wide(ring_job(c, J_H1 + o), split_job(c, S_H1 + o), wide_slot(par, S_H1 + o), ACT.Gelu, scales[:, 2, o:o + 1])
                        else:
                            take(ring_job(c, J_H1 + o), whole["act2"][:, o], ACT.Gelu, scales[:, 2, o:o + 1], hidden1_ready)
                    if more:
                        turned_rows(c + 1, 1 - par, exact)
                    for o in range(KH):
                        if exact:
                            slot = wide_slot(par, S_H2 + o - (0 if more else KD))
                            take_wide(ring_job(c, J_H2 + o), split_job(c, S_H2 + o), slot, ACT.Gelu, scales[:, 3, o:o + 1])
                        else:
                            take(ring_job(c, J_H2 + o), whole["act1"][:, o], ACT.Gelu, scales[:, 3, o:o + 1], hidden2_ready)

                if exact:
                    nc.scalar.activation(rounded["w1"][:], full["w1"][:], ACT.Copy).then_inc(rounded_act, 1)
                turned_rows(0, 0, exact)
                pass_a_over(act)
                bodies_b(act, body)

            on_flag(act, pass_b)

        @block.vector
        def _(dve):
            dve.wait_ge(weights_in, 16 * 11)
            dve.wait_ge(setup, 10)
            dve.wait_ge(a_ready, 1)
            nc.vector.tensor_scalar(neg_a[:], neg_a[:], -1.0, None, ALU.mult)
            for e in range(ET):
                for k in range(TAPS):
                    nc.vector.tensor_scalar(conv_diag[:, e, k], ident[:], conv_w_sb[:, e, k:k + 1], None, ALU.mult)
                last = nc.vector.tensor_scalar(d_diag[:, e], ident[:], d_sb[:, e:e + 1], None, ALU.mult)
            last.then_inc(diag_ready, 1)

            def norm(c, par, n):
                if n == DVE_AT["stats"]:
                    dve.wait_ge(x_in, 16 * (c + 1))
                    for q in range(NT):
                        last = nc.vector.bn_stats(bn[:, q], x_sb[:, par, q])
                    last.then_inc(bn_done, 1)
                    dve.wait_ge(setup, 10)
                    dve.wait_ge(bn_done, c + 1)
                    for q in range(NT):
                        last = nc.vector.bn_aggr(mv[:, q], bn[:, q])
                    last.then_inc(stats_ready, 1)
                if n == DVE_AT["normalize"]:
                    dve.wait_ge(rstd_ready, c + 1)
                    for q in range(NT):
                        last = nc.vector.tensor_scalar(xn[:, q], x_sb[:, par, q], mv[:, q, 0:1], rstd[:, q:q + 1],
                                                       ALU.subtract, ALU.mult)
                    last.then_inc(xn_ready, 1)

            def front(c, par, n):
                if n in DVE_AT["conv"]:
                    j = DVE_AT["conv"].index(n)
                    dve.wait_ge(front_full, front_job(c, F_CONV + j) + 1)
                    for i in range(2):
                        e = 2 * j + i
                        last = nc.vector.tensor_scalar(xc[:, e], front_bank(F_CONV + j)[:, i * T:(i + 1) * T], conv_b_sb[:, e:e + 1],
                                                       LOW, ALU.add, ALU.max)
                    last.then_inc(front_taken["dve"], 1)
                if n == DVE_AT["silu"]:
                    dve.wait_ge(silu_step, 3 * c + 3)
                    nc.vector.tensor_tensor(xc[:], xc[:], sig[:], ALU.mult).then_inc(xc_ready, 1)
                if n == DVE_AT["z"]:
                    wait_taken(dve, c, F_DT)
                    nc.vector.tensor_scalar(soft[:], z[:], HIGH, None, ALU.min).then_inc(zmin_ready, 1)
                if n == DVE_AT["dt"]:
                    dve.wait_ge(soft_step, 2 * c + 2)
                    nc.vector.tensor_tensor(dt[:, par], z[:], soft[:], ALU.max).then_inc(dt_ready, 1)

            def post(c, par, n):
                if n == DVE_AT["gate_low"]:
                    for q in range(NT):
                        dve.wait_ge(y_added[q], NS * (c + 1))
                    nc.vector.tensor_scalar(g[:], acc[:, par], LOW, None, ALU.max).then_inc(gm_ready, 1)
                if n == DVE_AT["gate"]:
                    dve.wait_ge(gate_step, 3 * c + 3)
                    nc.vector.tensor_tensor(g[:], g[:], gsig[:], ALU.mult).then_inc(g_ready, 1)
                if n == DVE_AT["x1"]:
                    dve.wait_ge(y_out_full, c + 1)
                    dve.wait_ge(xres_in, 16 * (c + 1))
                    after(dve, x1_out, 16 * (c - 1))
                    nc.vector.tensor_tensor(x1_sb[:, par].rearrange("p n d -> p (n d)"), post_bank,
                                            x_res[:, par].rearrange("p n d -> p (n d)"), ALU.add).then_inc(x1_ready, 1)

            def stats_b(c, par):
                dve.wait_ge(xb_in, 16 * (c + 1))
                for q in range(NTB):
                    last = nc.vector.bn_stats(bn_b[:, q], xb[:, par, q])
                last.then_inc(bn_b_done, 1)
                dve.wait_ge(setup, 10)
                dve.wait_ge(bn_b_done, c + 1)
                for q in range(NTB):
                    last = nc.vector.bn_aggr(mv_b[:, q], bn_b[:, q])
                last.then_inc(stats_b_ready, 1)

            def normalize_b(c, par):
                dve.wait_ge(rstd_b_ready, c + 1)
                for q in range(NTB):
                    last = nc.vector.tensor_scalar(xn_b[:, q], xb[:, par, q], mv_b[:, q, 0:1], rstd_b[:, q:q + 1],
                                                   ALU.subtract, ALU.mult)
                last.then_inc(xn_b_ready, 1)

            def scan(c, par, between, more):
                def recur(n):
                    dve.wait_ge(decay_ready, NS * c + n + 1)
                    dve.wait_ge(ub_ready, NS * c + n + 1)
                    for q in range(NT):
                        after(dve, turn_full[q], NS * c + n - 1)
                    after(dve, carry_ready, NS * c + n - 1)
                    nc.vector.tensor_tensor_scan(h[:, n % 2].rearrange("p e t -> p (e t)"), decay[:, n % 2].rearrange("p e t -> p (e t)"),
                                                 ub[:, n % 2].rearrange("p e t -> p (e t)"), 0.0, ALU.mult, ALU.add).then_inc(scan_done, 1)

                def add_y(n):
                    for q in range(NT):
                        if n == 0:
                            wait_taken(dve, c, F_ACC + q)
                        dve.wait_ge(turn_full[q], NS * c + n + 1)
                        after(dve, y_added[q], NS * c + n)
                        nc.vector.scalar_tensor_tensor(out=acc[:, par, q], in0=turned[n % 2][q], scalar=c_tok[:, par, q, n:n + 1], in1=acc[:, par, q],
                                                       op0=ALU.mult, op1=ALU.add).then_inc(y_added[q], 1)

                recur(0)
                for n in range(NS):
                    if n + 1 < NS:
                        recur(n + 1)
                    add_y(n)
                    between(n)
                    if last_body(c) and n == B_FIRST["stats"]:
                        stats_b(0, 0)
                    if last_body(c) and n == B_FIRST["normalize"]:
                        normalize_b(0, 0)
                    if isinstance(c, int) and c == 1 and n == 1:
                        dve.wait_ge(count_ready, 1)
                        nc.vector.tensor_copy(flag[:], post_bank[0:1, 0:1]).then_inc(flag_ready, 1)
                    if isinstance(c, int) and c == 0 and n >= 2:
                        look_at_weights(2 * (n - 2))
                        look_at_weights(2 * (n - 2) + 1)

            pieces = [full[name][:].rearrange("p k n -> p (k n)")[:, at:at + PIECE].bitcast(I32)
                      for name, shape in mlp_shapes.items() for at in range(0, shape[1] * shape[2], PIECE)]
            assert len(pieces) + 2 <= 2 * NS - 2 and len(pieces) + 3 == FLAG_STEPS

            def look_at_weights(step):
                if step == 0:
                    dve.wait_ge(mlp_weights_in, 16 * 10)
                    nc.vector.tensor_tensor(low_bits, pieces[0], pieces[1], ALU.bitwise_or).then_inc(flag_step, 1)
                    nc.vector.memset(ones[:], 1.0).then_inc(flag_step, 1)
                    return
                last_or = len(pieces) - 2
                if step > last_or + 3:
                    return
                dve.wait_ge(flag_step, step + 1)
                if step <= last_or:
                    nc.vector.tensor_tensor(low_bits, low_bits, pieces[step + 1], ALU.bitwise_or).then_inc(flag_step, 1)
                elif step == last_or + 1:
                    nc.vector.tensor_scalar(low_bits, low_bits, LOW_MASK, None, ALU.bitwise_and).then_inc(flag_step, 1)
                elif step == last_or + 2:
                    nc.vector.tensor_reduce(low_found[:], low_bits, mybir.AxisListType.X, ALU.max).then_inc(flag_step, 1)
                else:
                    nc.vector.tensor_scalar(not_exact[:], low_found[:], 0.0, None, ALU.not_equal).then_inc(flag_step, 1)

            bodies(norm, front, scan, post, lambda: None, dve)

            dve.wait_ge(mlp_weights_in, 16 * 10)

            def gate(c, par, o, exact):
                bank, place, of_bank = ring_job(c, J_L1 + 2 * o + 1)
                dve.wait_ge(silu_b_ready, KH * c + o + 1)
                dve.wait_ge(ring_full, place + 1)
                if exact:
                    row = split_job(c, o)
                    after(dve, rows_split, row - WIDE + 1)
                    dst = wide[:, wide_slot(par, o)]
                else:
                    dst = whole["act1"][:, o]
                nc.vector.scalar_tensor_tensor(out=dst, in0=ring[bank], scalar=scales[:, 1, o:o + 1], in1=silu_b[:, o % 2],
                                               op0=ALU.mult, op1=ALU.mult).then_inc(ring_taken[bank], 1)
                dve.wait_ge(ring_taken[bank], of_bank + 1)
                dve.sem_inc(wide_ready if exact else gated_ready, 1)

            def take_high(row, slot, dst):
                dve.wait_ge(wide_ready, row + 1)
                nc.vector.tensor_copy(dst, wide[:, slot]).then_inc(high_ready, 1)

            def take_low(row, slot, high_part, dst):
                dve.wait_ge(high_ready, row + 1)
                nc.vector.tensor_tensor(dst, wide[:, slot], high_part.bitcast(F32), ALU.subtract).then_inc(rows_split, 1)

            def split(name, o, row, slot):
                take_high(row, slot, high[name][:, o])
                take_low(row, slot, high[name][:, o], low[name][:, o])

            def split_turned(c, par):
                for d in range(KD):
                    split("xnT_b", d, split_turn(c, d), wide_turn_slot(par, d))

            def low_gated(c, par, o):
                take_low(split_job(c, o), wide_slot(par, o), high["act1"][:, o], low["act1"][:, o])

            def pass_b(exact):
                def body(c, par, more):
                    for o in range(KH):
                        gate(c, par, o, exact)
                        if exact and o >= 1:
                            low_gated(c, par, o - 1)
                        if exact and isinstance(c, int) and c == 0:
                            nc.vector.tensor_copy(rounded["h1"][:, o], full["h1"][:, o]).then_inc(rounded_dve, 1)
                    if exact:
                        low_gated(c, par, KH - 1)
                    if more:
                        stats_b(c + 1, 1 - par)
                    for o in range(KH):
                        if more and o == 3:
                            normalize_b(c + 1, 1 - par)
                        if exact:
                            split("act2", o, split_job(c, S_H1 + o), wide_slot(par, S_H1 + o))
                    if exact:
                        if more:
                            split_turned(c + 1, 1 - par)
                        for o in range(KH):
                            split("act1", o, split_job(c, S_H2 + o), wide_slot(par, S_H2 + o - (0 if more else KD)))
                    for j in range(NTB // 2):
                        bank, place, of_bank = ring_job(c, J_OUT + j)
                        dve.wait_ge(ring_full, place + 1)
                        nc.vector.tensor_tensor(prod_b[:, 2 * j:2 * j + 2], ring[bank].rearrange("p (n d) -> p n d", n=2),
                                                s3_row[:].rearrange("p (o d) -> p o d", o=1).to_broadcast([P, 2, DIM]),
                                                ALU.mult).then_inc(ring_taken[bank], 1)
                        dve.wait_ge(ring_taken[bank], of_bank + 1)
                    after(dve, out_stored, 16 * (c - 1))
                    nc.vector.tensor_tensor(out_sb[:, par], prod_b[:], xb[:, par], ALU.add).then_inc(out_ready, 1)

                if exact:
                    nc.vector.tensor_copy(rounded["w2"][:], full["w2"][:]).then_inc(rounded_dve, 1)
                    split_turned(0, 0)
                pass_a_over(dve)
                bodies_b(dve, body)

            on_flag(dve, pass_b)

        @block.tensor
        def _(pe):
            pe.wait_ge(weights_in, 16 * 11)
            pe.wait_ge(setup, 10)
            pe.wait_ge(diag_ready, 1)

            def select(row):
                return ident[:, row:row + 1].to_broadcast([P, P])

            def norm(c, par, n):
                if n == PE_AT["xn"]:
                    wait_taken(pe, c, F_XN - 2)
                    pe.wait_ge(xn_ready, c + 1)
                    for q in range(NT):
                        for d in range(KD):
                            last = nc.tensor.transpose(front_bank(F_XN)[:, d * T + q * P:d * T + (q + 1) * P], xn[:, q, d * P:(d + 1) * P], ident[:])
                    last.then_inc(front_full, 1)
                if n == PE_AT["next_xp"] and not first_norm(c):
                    wait_taken(pe, c, F_XN)
                    project(c, 0)

            def project(c, j):
                wait_taken(pe, c, F_XP + j - 2)
                for i in range(2):
                    e = 2 * j + i
                    for d in range(KD):
                        last = nc.tensor.matmul(front_bank(F_XP + j)[:, i * T:(i + 1) * T], w_in_sb[:, d, e * P:(e + 1) * P], xnT[:, d],
                                                start=(d == 0), stop=(d == KD - 1))
                last.then_inc(front_full, 1)

            def convolve(c, j, i):
                if i == 0:
                    wait_taken(pe, c, F_CONV + j - 2)
                    wait_taken(pe, c, F_XP + j)
                e = 2 * j + i
                for tap in range(TAPS):
                    last = nc.tensor.matmul(front_bank(F_CONV + j)[:, i * T:(i + 1) * T], conv_diag[:, e, tap], xp[:, e, tap:tap + T],
                                            start=(tap == 0), stop=(tap == TAPS - 1))
                if i == 1:
                    last.then_inc(front_full, 1)

            def front(c, par, n):
                if n == PE_AT["xp"]:
                    if first_norm(c):
                        wait_taken(pe, c, F_XN)
                        project(c, 0)
                    project(c, 1)
                for j in range(2):
                    for i in range(2):
                        if n == PE_AT["conv"][j][i]:
                            convolve(c, j, i)
                if n == PE_AT["ssm"]:
                    front_work(c, par, F_SSM)
                if n == PE_AT["dt"]:
                    front_work(c, par, F_DT)
                if n == PE_AT["c"]:
                    front_work(c, par, F_C)
                if n in PE_AT["acc"]:
                    front_work(c, par, F_ACC + PE_AT["acc"].index(n))

            def front_work(c, par, job):
                bank = front_bank(job)
                wait_taken(pe, c, job - 2)
                if job == F_SSM:
                    pe.wait_ge(xc_ready, c + 1)
                    for e in range(ET):
                        last = nc.tensor.matmul(bank[:, 0:T], w_x_sb[:, e], xc[:, e], start=(e == 0), stop=(e == ET - 1))
                elif job == F_DT:
                    wait_taken(pe, c, F_SSM)
                    last = nc.tensor.matmul(bank[:, 0:T], select(ROW_DT), ssm[:, par], start=True, stop=True)
                elif job == F_C:
                    for q in range(NT):
                        last = nc.tensor.transpose(bank[:, q * P:(q + 1) * P], ssm[:, par, q * P:(q + 1) * P], ident[:])
                else:
                    q = job - F_ACC
                    for d in range(KD):
                        nc.tensor.matmul(bank, xnT[:, d, q * P:(q + 1) * P], w_in_sb[:, d, DI:2 * DI], start=(d == 0), stop=False)
                    for e in range(ET):
                        last = nc.tensor.matmul(bank[:, e * P:(e + 1) * P], xc[:, e, q * P:(q + 1) * P], d_diag[:, e],
                                                start=False, stop=(e == ET - 1))
                last.then_inc(front_full, 1)

            def post(c, par, n):
                if n in PE_AT["gT"]:
                    j = PE_AT["gT"].index(n)
                    if j == 0:
                        pe.wait_ge(g_ready, c + 1)
                        after(pe, x1_ready, c)
                    else:
                        pe.wait_ge(gT_ready, 2 * c + 1)
                    for i in range(2):
                        e = 2 * j + i
                        for q in range(NT):
                            last = nc.tensor.transpose(post_bank[:, i * T + q * P:i * T + (q + 1) * P], g[:, q, e * P:(e + 1) * P], ident[:])
                    last.then_inc(g_turned, 1)
                if n in PE_AT["out"]:
                    q = PE_AT["out"].index(n)
                    if q == 0:
                        pe.wait_ge(gT_ready, 2 * (c + 1))
                    for e in range(ET):
                        last = nc.tensor.matmul(post_bank[:, q * DIM:(q + 1) * DIM], gT[:, e, q * P:(q + 1) * P], w_out_sb[:, e],
                                                start=(e == 0), stop=(e == ET - 1))
                    if q == NT - 1:
                        last.then_inc(y_out_full, 1)

            def pair_rows(c, par, k):
                after(pe, pair_taken, PAIRS * c + k)
                for j in range(2):
                    last = nc.tensor.matmul(pair_bank[:, j * T:(j + 1) * T], select(ROW_B + 2 * k + j), ssm[:, par], start=True, stop=True)
                last.then_inc(pair_full, 1)

            def free(job):
                bank, place, of_bank = job
                after(pe, ring_taken[bank], of_bank)
                return ring[bank]

            def turn_rows(c):
                pe.wait_ge(xn_b_ready, c + 1)
                for d in range(KD):
                    bank = free(turn_job(c, d))
                    for q in range(NTB):
                        last = nc.tensor.transpose(bank[:, q * P:(q + 1) * P], xn_b[:, q, d * P:(d + 1) * P], ident[:])
                    last.then_inc(ring_full, 1)

            def scan(c, par, between, more):
                if isinstance(c, int) and c == 0:
                    pair_rows(0, 0, 2)
                for n in range(NS):
                    pe.wait_ge(scan_done, NS * c + n + 1)
                    for q in range(NT):
                        after(pe, y_added[q], NS * c + n - 1)
                        for e in range(ET):
                            last = nc.tensor.transpose(turned[n % 2][q][:, e * P:(e + 1) * P], h[:, n % 2, e, 1 + q * P:1 + (q + 1) * P], ident[:])
                        last.then_inc(turn_full[q], 1)
                    between(n)
                    if n % 2 == 1:
                        k = (n + 5) // 2
                        if k < PAIRS:
                            pair_rows(c, par, k)
                        elif more:
                            pair_rows(c + 1, 1 - par, k - PAIRS)
                    if last_body(c) and n == B_FIRST["turn"]:
                        wait_taken(pe, c, F_ACC)
                        wait_taken(pe, c, F_ACC + 1)
                        turn_rows(0)
                if isinstance(c, int) and c == 0:
                    pe.wait_ge(flag_step, FLAG_STEPS)
                    nc.tensor.matmul(post_bank[0:1, 0:1], not_exact[:], ones[:], start=True, stop=True).then_inc(count_ready, 1)

            def start():
                pair_rows(0, 0, 0)
                pair_rows(0, 0, 1)

            bodies(norm, front, scan, post, start, pe)

            pe.wait_ge(mlp_weights_in, 16 * 10)

            def pass_b(exact):
                def weights_of(name):
                    return rounded[name] if exact else full[name]

                def parts_of(name):
                    return (high[name], low[name]) if exact else (whole[name],)

                def wait_row(c, k, first_split, rows_ready):
                    if exact:
                        pe.wait_ge(rows_split, split_job(c, first_split + k) + 1)
                    else:
                        pe.wait_ge(rows_ready, KH * c + k + 1)

                def layer(c, job0, weights, rows, first_split, rows_ready):
                    first = RING // 2
                    tiles = [list(range(first))] + [[o] for o in range(first, KH)]
                    parts = parts_of(rows)
                    for group in tiles:
                        banks_of = [free(ring_job(c, job0 + o)) for o in group]
                        for k in range(KH):
                            if group[0] == 0:
                                wait_row(c, k, first_split, rows_ready)
                            for o, bank in zip(group, banks_of):
                                for i, part in enumerate(parts):
                                    last = nc.tensor.matmul(bank, weights[:, k, o * P:(o + 1) * P], part[:, k],
                                                            start=(k + i == 0), stop=(k == KH - 1 and i == len(parts) - 1))
                                if k == KH - 1:
                                    last.then_inc(ring_full, 1)

                def body(c, par, more):
                    if exact:
                        pe.wait_ge(rows_split, split_turn(c, KD - 1) + 1)
                    else:
                        pe.wait_ge(xnT_b_ready, KD * (c + 1))
                    parts = parts_of("xnT_b")
                    for o in range(KH):
                        for j, weights in enumerate((weights_of("w1"), weights_of("w2"))):
                            bank = free(ring_job(c, J_L1 + 2 * o + j))
                            for d in range(KD):
                                for i, part in enumerate(parts):
                                    last = nc.tensor.matmul(bank, weights[:, d, o * P:(o + 1) * P], part[:, d],
                                                            start=(d + i == 0), stop=(d == KD - 1 and i == len(parts) - 1))
                            last.then_inc(ring_full, 1)
                    if exact and isinstance(c, int) and c == 0:
                        pe.wait_ge(rounded_dve, 1 + KH)
                    layer(c, J_H1, weights_of("h1"), "act1", 0, gated_ready)
                    if more:
                        turn_rows(c + 1)
                    if exact and isinstance(c, int) and c == 0:
                        pe.wait_ge(rounded_pool, 1)
                    layer(c, J_H2, weights_of("h2"), "act2", S_H1, hidden1_ready)
                    banks_of = [free(ring_job(c, J_OUT + j)) for j in range(NTB // 2)]
                    parts = parts_of("act1")
                    w3_of = weights_of("w3")
                    if exact and isinstance(c, int) and c == 0:
                        pe.wait_ge(rounded_pool, 2)
                    for half in range(2):
                        for k in range(KH):
                            if half == 0:
                                wait_row(c, k, S_H2, hidden2_ready)
                            for j, bank in enumerate(banks_of):
                                q = 2 * j + half
                                for i, part in enumerate(parts):
                                    last = nc.tensor.matmul(bank[:, half * DIM:(half + 1) * DIM], part[:, k, q * P:(q + 1) * P], w3_of[:, k],
                                                            start=(k + i == 0), stop=(k == KH - 1 and i == len(parts) - 1))
                                if half == 1 and k == KH - 1:
                                    last.then_inc(ring_full, 1)

                if exact:
                    pe.wait_ge(rounded_act, 1)
                    pe.wait_ge(rounded_dve, 1)
                bodies_b(pe, body)

            on_flag(pe, pass_b)


_INS = ["x", "w_in", "conv_w", "conv_b", "w_x", "w_dt", "b_dt", "a_log", "d_skip", "w_out",
        "w1", "s1", "w2", "s2", "h1", "t1", "h2", "t2", "w3", "s3"]


def kernel(**inputs):
    import numpy as np
    import concourse.bacc as bacc
    from concourse.bass_utils import run_bass_kernel_spmd

    a = {k[3:]: np.asarray(v) for k, v in inputs.items()}

    def turn(w):
        return np.ascontiguousarray(w.T)

    def columns(v):
        return np.ascontiguousarray(v.reshape(-1, P).T)

    arrays = {
        "x": a["attn_x"], "w_in": turn(a["attn_W_in"]), "conv_w": a["attn_conv_w"], "conv_b": columns(a["attn_conv_b"]),
        "w_x": turn(a["attn_W_x"]), "w_dt": columns(a["attn_W_dt"]), "b_dt": columns(a["attn_b_dt"]),
        "a_log": a["attn_A_log"], "d_skip": columns(a["attn_D"]), "w_out": turn(a["attn_W_out"]),
        "w1": turn(a["ffn_w1_w"]), "s1": columns(a["ffn_w1_s"]), "w2": turn(a["ffn_w2_w"]), "s2": columns(a["ffn_w2_s"]),
        "h1": turn(a["ffn_h1_w"]), "t1": columns(a["ffn_h1_s"]), "h2": turn(a["ffn_h2_w"]), "t2": columns(a["ffn_h2_s"]),
        "w3": turn(a["ffn_w3_w"]), "s3": a["ffn_w3_s"],
    }
    nc = bacc.Bacc("TRN2", target_bir_lowering=False, num_devices=1)
    args = [nc.dram_tensor(f"in_{k}", arrays[k].shape, mybir.dt.from_np(arrays[k].dtype), kind="ExternalInput").ap() for k in _INS]
    x1 = nc.dram_tensor("x1_scratch", arrays["x"].shape, F32, kind="Internal").ap()
    out = nc.dram_tensor("out", arrays["x"].shape, F32, kind="ExternalOutput").ap()
    program(nc, *args, x1, out)
    r = run_bass_kernel_spmd(nc, [{f"in_{k}": arrays[k] for k in _INS}], core_ids=[0])
    return r.results[0]["out"]
```
